# Optimizing a Trainium2 kernel written in Bass

```python
import numpy as np
import jax
import jax.numpy as jnp

def _softmax(x, axis=-1):
    return jax.nn.softmax(x, axis=axis)

def _gelu(x):
    return jax.nn.gelu(x, approximate=True)

def _silu(x):
    return jax.nn.silu(x)

def _sigmoid(x):
    return jax.nn.sigmoid(x)

def _layernorm(x, axis=-1, eps=1e-05):
    m = jnp.mean(x, axis=axis, keepdims=True)
    v = jnp.var(x, axis=axis, keepdims=True)
    return (x - m) / jnp.sqrt(v + eps)

def _scatter_add(tgt, idx, src, axis=0):
    return tgt.at[idx].add(src)

def _segment_sum(src, seg, n):
    return jax.ops.segment_sum(src, seg, n)
kernel_name = 'mk_cond_resid_d4_seqx_r4_557a2e'

def setup_inputs(seed: int=0):
    np.random.seed(seed)
    _w = jnp.asarray

    def _rec_inputs():
        import jax
        import jax.numpy as jnp
        _rk = jax.random.key(seed)
        x = 7.22e-05 + 1 * jax.random.normal(jax.random.fold_in(_rk, 1), (8, 256, 256), jnp.float32)
        _lenS = 256 - jax.random.randint(jax.random.fold_in(_rk, 7), (8,), 0, max(1, 256 // 4) + 1, jnp.int32)
        _lenS2 = 256 - jax.random.randint(jax.random.fold_in(_rk, 8), (8,), 0, max(1, 256 // 4) + 1, jnp.int32)
        itok_B_0_2 = jax.random.randint(jax.random.fold_in(_rk, 11), (8,), 0, 3, jnp.int32)
        fside_Bx8_0 = jax.random.uniform(jax.random.fold_in(_rk, 12), (8, 8), jnp.float32, 0.0, 0.556406)
        condB_sharedgateprob = jax.random.uniform(jax.random.fold_in(_rk, 13), (8,), jnp.float32, 0.0, 0.794948)
        itok_B_0_8 = jax.random.randint(jax.random.fold_in(_rk, 14), (8,), 0, 9, jnp.int32)
        itok_B_0_7 = jax.random.randint(jax.random.fold_in(_rk, 15), (8,), 0, 8, jnp.int32)
        return (x, itok_B_0_2, fside_Bx8_0, condB_sharedgateprob, itok_B_0_8, itok_B_0_7)
    x, itok_B_0_2, fside_Bx8_0, condB_sharedgateprob, itok_B_0_8, itok_B_0_7 = _rec_inputs()

    def _L0_cond_setup():
        import jax, jax.numpy as jnp
        import numpy as np
        B, S, D, F, E = (8, 256, 256, 1024, 4)

        def _dense(x, wi, wo):
            return jax.nn.relu(x @ wi) @ wo
        key = jax.random.key(seed)
        ks = jax.random.split(key, 10)
        scale = 0.02
        return {'hidden_states': jax.random.normal(ks[0], (B, S, D), jnp.float32), 'type_idx': jax.random.randint(ks[1], (B,), 0, 3, jnp.int32), 'expert_wi': jax.random.normal(ks[2], (E, D, F), jnp.float32) * scale, 'expert_wo': jax.random.normal(ks[3], (E, F, D), jnp.float32) * scale, 'share_wi': jax.random.normal(ks[4], (3, D, F), jnp.float32) * scale, 'share_wo': jax.random.normal(ks[5], (3, F, D), jnp.float32) * scale, 'gate_vecs': jnp.array([[0.22, 0.22, 0.2, 0.2], [0.2, 0.22, 0.22, 0.2], [0.2, 0.2, 0.22, 0.22]], jnp.float32), 'gate_w1': jax.random.normal(ks[6], (4 * D, D), jnp.float32) * scale, 'gate_w2': jax.random.normal(ks[7], (D, 4), jnp.float32) * scale}
    _L0_cond_all = _L0_cond_setup()
    _L0_cond_in = {k: v for k, v in _L0_cond_all.items() if k in ('expert_wi', 'expert_wo', 'share_wi', 'share_wo', 'gate_vecs', 'gate_w1', 'gate_w2')}
    del _L0_cond_all

    def _L1_cond_setup():
        import jax, jax.numpy as jnp
        import numpy as np
        E, B, S, D, F = (8, 2, 256, 256, 1024)
        key = jax.random.key(seed)
        ks = jax.random.split(key, 9)
        sc_d = 1.0 / np.sqrt(D)
        sc_f = 1.0 / np.sqrt(F)
        hidden_states = jax.random.normal(ks[0], (B, S, D), dtype=jnp.float32)
        gating_probs = jax.nn.softmax(jax.random.normal(ks[1], (B, E), dtype=jnp.float32), axis=-1)
        shared_gate_prob = jax.nn.sigmoid(jax.random.normal(ks[2], (B, 1), dtype=jnp.float32))
        Wg = jax.random.normal(ks[3], (E, D, F), dtype=jnp.float32) * sc_d
        Wu = jax.random.normal(ks[4], (E, D, F), dtype=jnp.float32) * sc_d
        Wd = jax.random.normal(ks[5], (E, F, D), dtype=jnp.float32) * sc_f
        Sg = jax.random.normal(ks[6], (D, F), dtype=jnp.float32) * sc_d
        Su = jax.random.normal(ks[7], (D, F), dtype=jnp.float32) * sc_d
        Sd = jax.random.normal(ks[8], (F, D), dtype=jnp.float32) * sc_f
        return {'hidden_states': hidden_states, 'gating_probs': gating_probs, 'shared_gate_prob': shared_gate_prob, 'Wg': Wg, 'Wu': Wu, 'Wd': Wd, 'Sg': Sg, 'Su': Su, 'Sd': Sd}
    _L1_cond_all = _L1_cond_setup()
    _L1_cond_in = {k: v for k, v in _L1_cond_all.items() if k in ('Wg', 'Wu', 'Wd', 'Sg', 'Su', 'Sd')}
    del _L1_cond_all

    def _L2_cond_setup():
        import jax, jax.numpy as jnp
        import numpy as np
        LN_EPS = 1e-05
        key = jax.random.key(seed)
        ks = jax.random.split(key, 8)
        B, S, H, A, L = (32, 512, 256, 64, 10)
        return {'hidden_states': jax.random.normal(ks[0], (B, S, H), dtype=jnp.float32), 'language_ids': jax.random.randint(ks[1], (B,), 0, L, dtype=jnp.int64), 'W1': jax.random.normal(ks[2], (L, H, A), dtype=jnp.float32) * (1.0 / np.sqrt(H)), 'b1': jnp.zeros((L, A), dtype=jnp.float32), 'W2': jax.random.normal(ks[3], (L, A, H), dtype=jnp.float32) * (1.0 / np.sqrt(A)), 'b2': jnp.zeros((L, H), dtype=jnp.float32), 'gamma': jnp.ones((L, H), dtype=jnp.float32), 'beta': jnp.zeros((L, H), dtype=jnp.float32)}
    _L2_cond_all = _L2_cond_setup()
    _L2_cond_in = {k: v for k, v in _L2_cond_all.items() if k in ('W1', 'b1', 'W2', 'b2', 'gamma', 'beta')}
    del _L2_cond_all

    def _L3_cond_setup():
        import jax, jax.numpy as jnp
        import numpy as np
        S, O, H = (8, 256, 256)
        B, N = (32, 128)
        key = jax.random.key(seed)
        k1, k2, k3, k4 = jax.random.split(key, 4)
        x = jax.random.normal(k1, (B, N, H), dtype=jnp.float32)
        subject_id = jax.random.randint(k2, (B,), 0, S)
        wbound = jnp.sqrt(2.0 / 6.0) * jnp.sqrt(3.0 / H)
        weight = jax.random.uniform(k3, (S, O, H), minval=-wbound, maxval=wbound, dtype=jnp.float32)
        bbound = 1.0 / jnp.sqrt(H)
        bias = jax.random.uniform(k4, (S, O), minval=-bbound, maxval=bbound, dtype=jnp.float32)
        return {'x': x, 'subject_id': subject_id, 'weight': weight, 'bias': bias}
    _L3_cond_all = _L3_cond_setup()
    _L3_cond_in = {k: v for k, v in _L3_cond_all.items() if k in ('weight', 'bias')}
    del _L3_cond_all
    return {'x': x, 'itok_B_0_2': itok_B_0_2, 'fside_Bx8_0': fside_Bx8_0, 'condB_sharedgateprob': condB_sharedgateprob, 'itok_B_0_8': itok_B_0_8, 'itok_B_0_7': itok_B_0_7, 'L0_cond_expert_wi': _L0_cond_in['expert_wi'], 'L0_cond_expert_wo': _L0_cond_in['expert_wo'], 'L0_cond_share_wi': _L0_cond_in['share_wi'], 'L0_cond_share_wo': _L0_cond_in['share_wo'], 'L0_cond_gate_vecs': _L0_cond_in['gate_vecs'], 'L0_cond_gate_w1': _L0_cond_in['gate_w1'], 'L0_cond_gate_w2': _L0_cond_in['gate_w2'], 'L1_cond_Wg': _L1_cond_in['Wg'], 'L1_cond_Wu': _L1_cond_in['Wu'], 'L1_cond_Wd': _L1_cond_in['Wd'], 'L1_cond_Sg': _L1_cond_in['Sg'], 'L1_cond_Su': _L1_cond_in['Su'], 'L1_cond_Sd': _L1_cond_in['Sd'], 'L2_cond_W1': _L2_cond_in['W1'], 'L2_cond_b1': _L2_cond_in['b1'], 'L2_cond_W2': _L2_cond_in['W2'], 'L2_cond_b2': _L2_cond_in['b2'], 'L2_cond_gamma': _L2_cond_in['gamma'], 'L2_cond_beta': _L2_cond_in['beta'], 'L3_cond_weight': _L3_cond_in['weight'], 'L3_cond_bias': _L3_cond_in['bias']}

def reference(x, itok_B_0_2, fside_Bx8_0, condB_sharedgateprob, itok_B_0_8, itok_B_0_7, L0_cond_expert_wi, L0_cond_expert_wo, L0_cond_share_wi, L0_cond_share_wo, L0_cond_gate_vecs, L0_cond_gate_w1, L0_cond_gate_w2, L1_cond_Wg, L1_cond_Wu, L1_cond_Wd, L1_cond_Sg, L1_cond_Su, L1_cond_Sd, L2_cond_W1, L2_cond_b1, L2_cond_W2, L2_cond_b2, L2_cond_gamma, L2_cond_beta, L3_cond_weight, L3_cond_bias):
    import jax
    import jax.numpy as jnp

    def _L0_cond_ref(hidden_states, type_idx, expert_wi, expert_wo, share_wi, share_wo, gate_vecs, gate_w1, gate_w2):
        import jax, jax.numpy as jnp
        import numpy as np
        B, S, D, F, E = (8, 256, 256, 1024, 4)

        def _dense(x, wi, wo):
            return jax.nn.relu(x @ wi) @ wo
        s0 = _dense(hidden_states, share_wi[0], share_wo[0])
        s1 = _dense(hidden_states, share_wi[1], share_wo[1])
        s2 = _dense(hidden_states, share_wi[2], share_wo[2])
        idx_a = type_idx
        idx_b = type_idx + 1
        out_a = jnp.einsum('bsf,bfd->bsd', jax.nn.relu(jnp.einsum('bsd,bdf->bsf', hidden_states, expert_wi[idx_a])), expert_wo[idx_a])
        out_b = jnp.einsum('bsf,bfd->bsd', jax.nn.relu(jnp.einsum('bsd,bdf->bsf', hidden_states, expert_wi[idx_b])), expert_wo[idx_b])
        p = jax.nn.softmax(gate_vecs / 0.1, axis=-1)
        wa = p[type_idx, idx_a][:, None, None]
        wb = p[type_idx, idx_b][:, None, None]
        expert_out = out_a * wa + out_b * wb
        gi = jnp.concatenate([expert_out[:, 0], s0[:, 0], s1[:, 0], s2[:, 0]], axis=-1)
        g = jax.nn.softmax(jax.nn.relu(gi @ gate_w1) @ gate_w2, axis=-1)
        out = expert_out * g[:, 0, None, None] + s0 * g[:, 1, None, None] + s1 * g[:, 2, None, None] + s2 * g[:, 3, None, None]
        return out

    def _L1_cond_ref(hidden_states, gating_probs, shared_gate_prob, Wg, Wu, Wd, Sg, Su, Sd):
        import jax, jax.numpy as jnp
        import numpy as np
        E, B, S, D, F = (8, 2, 256, 256, 1024)
        h = hidden_states
        g = jnp.einsum('bsd,edf->ebsf', h, Wg)
        u = jnp.einsum('bsd,edf->ebsf', h, Wu)
        expert_outs = jnp.einsum('ebsf,efd->ebsd', jax.nn.silu(g) * u, Wd)
        expert_output = jnp.einsum('be,ebsd->bsd', gating_probs, expert_outs)
        shared = jnp.einsum('bsf,fd->bsd', jax.nn.silu(h @ Sg) * (h @ Su), Sd)
        sg = shared_gate_prob[:, :, None]
        return (1.0 - sg) * expert_output + sg * shared

    def _L2_cond_ref(hidden_states, language_ids, W1, b1, W2, b2, gamma, beta):
        import jax, jax.numpy as jnp
        import numpy as np
        LN_EPS = 1e-05
        w1 = W1[language_ids]
        w2 = W2[language_ids]
        h = jnp.einsum('bsh,bha->bsa', hidden_states, w1) + b1[language_ids][:, None, :]
        h = jax.nn.relu(h)
        adapted = jnp.einsum('bsa,bah->bsh', h, w2) + b2[language_ids][:, None, :]
        x = hidden_states + adapted
        mean = jnp.mean(x, axis=-1, keepdims=True)
        var = jnp.mean(jnp.square(x - mean), axis=-1, keepdims=True)
        normed = (x - mean) * jax.lax.rsqrt(var + LN_EPS)
        return normed * gamma[language_ids][:, None, :] + beta[language_ids][:, None, :]

    def _L3_cond_ref(x, subject_id, weight, bias):
        import jax, jax.numpy as jnp
        import numpy as np
        S, O, H = (8, 256, 256)
        B, N = (32, 128)
        W = weight[subject_id]
        b = bias[subject_id]
        y = jnp.einsum('bnh,boh->bno', x, W) + b[:, None, :]
        return y
    x = x + _L0_cond_ref(x, itok_B_0_2, L0_cond_expert_wi, L0_cond_expert_wo, L0_cond_share_wi, L0_cond_share_wo, L0_cond_gate_vecs, L0_cond_gate_w1, L0_cond_gate_w2)
    x = x + _L1_cond_ref(x, fside_Bx8_0, condB_sharedgateprob[:, None], L1_cond_Wg, L1_cond_Wu, L1_cond_Wd, L1_cond_Sg, L1_cond_Su, L1_cond_Sd)
    x = x + _L2_cond_ref(x, itok_B_0_8, L2_cond_W1, L2_cond_b1, L2_cond_W2, L2_cond_b2, L2_cond_gamma, L2_cond_beta)
    x = x + _L3_cond_ref(x, itok_B_0_7, L3_cond_weight, L3_cond_bias)
    return x

_drawn_inputs = setup_inputs


def setup_inputs(seed=0):
    import zlib

    import numpy as np

    out = dict(_drawn_inputs(seed))
    spreads = {'L2_cond_b1': (0.0, 0.302),
     'L2_cond_b2': (0.0, 0.1),
     'L2_cond_gamma': (1.0, 0.2),
     'L2_cond_beta': (0.0, 0.1)}
    factors = {'L0_cond_expert_wi': 4.609,
     'L0_cond_expert_wo': 3.862,
     'L0_cond_gate_vecs': 8.0,
     'L0_cond_gate_w1': 8.0,
     'L0_cond_gate_w2': 8.0,
     'L3_cond_bias': 3.777}
    for name, (base, spread) in spreads.items():
        noise = np.random.default_rng([zlib.crc32(name.encode()), seed]).standard_normal(out[name].shape)
        drawn = base * np.exp(spread * noise) if base else spread * noise
        out[name] = jnp.asarray(drawn.astype(out[name].dtype))
    for name, factor in factors.items():
        out[name] = (out[name] * factor).astype(out[name].dtype)
    return out
```

```python
import concourse.bass as bass
from concourse import mybir
from contextlib import ExitStack


B, S, D, F = 8, 256, 256, 1024
P = 128
DT = D // P
FT = F // P
NB = 4
BLK = B * S // NB
NSH = 3
NE1 = 9
A2 = 64
CH = 1024
RAW = 4
L0_JOBS = [("shared", 0), ("expert", 0), ("shared", 1), ("expert", 1), ("shared", 2), ("expert", 2), ("expert", 3)]
NJ = len(L0_JOBS)
L0_STEPS = NJ * FT
L0_ALL = NB * L0_STEPS
EX_STEPS = 4 * FT
EX_CH = EX_STEPS // 2
SUMS = [0, 1, 0, 1, 0, 1, 2]
PLAIN0 = 4 + 4 * NSH


def job_of_expert(j):
    return [i for i, (kind, n) in enumerate(L0_JOBS) if kind == "expert" and n == j][0]


def early_exout(m, first, last_block):
    return first and m == 4 or last_block and m in (8, EX_CH - 1)


def local_step(k):
    return FT * job_of_expert(k // FT) + k % FT


def stream_table():
    sh = lambda j, m, h: ("plain", 1 + 4 * j + 2 * h + m)
    t = [("plain", 0), sh(0, 0, 0), sh(0, 1, 0), sh(0, 0, 1), sh(0, 1, 1),
         sh(1, 0, 0), sh(1, 1, 0), sh(1, 0, 1), ("expert", 0), ("expert", 1), ("expert", 2), ("expert", 3), ("expert", 4), ("expert", 5),
         sh(1, 1, 1)] + [sh(2, m, h) for h in range(2) for m in range(2)]
    t += [("plain", 13), ("plain", 14), ("plain", 15)]
    t += [("expert", q) for q in range(6, 58)]
    t += [("plain", PLAIN0 + r) for r in range(6)]
    t += [("expert", q) for q in range(58, 64)]
    t += [("plain", PLAIN0 + r) for r in range(6, 6 * NE1 + B)]
    return t


STREAM = stream_table()
AT = {k: c for c, k in enumerate(STREAM)}


def build(nc, xT_d, sh_d, ex_d, l1_d, types_d, types_row_d, gvec_d, gw1_d, gw2_d, prob_d, sgate_d, w1_d, w2_d, b1_d, cols_d, w3_d, bias_d, ident_d, out_d):
    f32, f32r, i32 = mybir.dt.float32, mybir.dt.float32r, mybir.dt.int32
    ALU, ACT, AX = mybir.AluOpType, mybir.ActivationFunctionType, mybir.AxisListType

    size = {f32: 4, f32r: 4, i32: 4}
    top = [(nc.sbuf_base + 31) // 32 * 32]

    def place(name, shape, dt, over=None, skip=0):
        n = size[dt]
        for s in shape[1:]:
            n *= s
        if over is None:
            at = top[0]
            top[0] += (n + 31) // 32 * 32
        else:
            at = where[over] + skip
        where[name] = at
        return nc.alloc_sbuf_tensor_at(name, shape, dt, offset=at)

    where = {}
    W = place("weights", [P, 6, 2, FT * D], f32r)
    raw = place("raw", [P, RAW, CH], f32)
    exin = place("expert_in", [P, 2, 2, 512], f32r)
    exout = place("expert_out", [P, 2, 2, 512], f32r)
    x = place("x", [P, DT, B * S], f32)
    xh = place("x_hi", [P, DT, B * S], f32r)
    xl = place("x_lo", [P, DT, B * S], f32r)
    acc = place("shared_sums", [P, NSH, DT, BLK], f32)
    hid = place("hidden", [P, 2, 2, BLK], f32r)
    gw1 = place("gate_w1", [P, 8, D], f32)
    gw2 = place("gate_w2", [P, 2, 4], f32)
    ident = place("ident", [P, P], f32)
    identr = place("ident_r", [P, P], f32r)
    ones = place("ones", [P, P], f32)
    types = place("types", [P, B], i32)
    typesf = place("types_f", [P, B], f32)
    idx = place("idx", [1, 3, B], i32)
    gvec = place("gate_vecs", [P, 3, 4], f32)
    gmax = place("gate_vec_max", [P, 3], f32)
    gp = place("gate_vec_probs", [P, 3, 4], f32)
    wab = place("expert_weight", [P, 2, B], f32)
    wtmp = place("expert_weight_part", [P, 2, B], f32)
    prob = place("prob", [P, B, NE1 - 1], f32)
    sg = place("shared_gate", [P, B], f32)
    omg = place("one_minus_gate", [P, B], f32)
    coef = place("l1_coef", [P, NE1, B], f32)
    r1 = place("gate_hidden", [P, 2, 2], f32)
    gprod = place("gate_products", [P, 2, 2, 4], f32)
    glmax = place("gate_logit_max", [P, 2], f32)
    gexp = place("gate_exp", [P, 2, 4], f32)
    gsum = place("gate_sum", [P, 2], f32)
    g = place("gate", [P, 2, 4], f32)
    cols = place("l2_cols", [P, B, 6], f32)
    b1 = place("l2_b1", [A2, B], f32)
    var = place("variance", [P, 4], f32)
    mhalf = place("minus_half", [P, 4], f32)
    rstd = place("rstd", [P, 4], f32)
    assert top[0] <= nc.sbuf_usable_end, (top[0], nc.sbuf_usable_end)
    sil = place("silu", [P, 2, BLK], f32, over="expert_in")
    gat = place("gated", [P, 2, BLK], f32, over="expert_in", skip=4 * 2 * BLK)
    ostage = place("out_stage", [P, 2, 4, D], f32, over="expert_out")
    biasb = place("l3_bias", [P, B, D], f32, over="shared_sums")
    diag = place("rstd_diag", [P, 4, P], f32, over="shared_sums", skip=4 * B * D)
    w1r = place("l2_w1", [P, B, 2, DT * A2], f32r, over="gate_w1")
    y = place("y", [P, DT, BLK], f32, over="raw")
    sq = place("squares", [P, DT, BLK], f32, over="raw", skip=4096)
    ru = place("l2_hidden", [A2, BLK], f32, over="raw", skip=8192)
    u = place("l2_hidden_r", [A2, 2, BLK], f32r, over="raw", skip=10240)
    w3 = W[:, 3:5].rearrange("p s h n -> p (s h n)").rearrange("p (b h n) -> p b h n", b=B, h=2)
    w2 = W[0:A2, 5].rearrange("p h n -> p (h n)").rearrange("p (b h n) -> p b h n", b=B, h=2)

    ctx = ExitStack()
    with ctx:
        def bank(name, n):
            return ctx.enter_context(nc.psum_tensor(name, [P, n, 512], f32))

        def sem(name):
            return ctx.enter_context(nc.semaphore(name))

        up_ps = bank("up", 2)
        up2_ps = bank("up2", 2)
        sums = [bank("sum0", 2), bank("sum1", 2), up2_ps]

        raw_full = [sem(f"raw_full{i}") for i in range(RAW)]
        const_full, gw1_full = sem("const_full"), sem("gw1_full")
        idx_full = sem("idx_full")
        consts = sem("consts")
        softp = sem("softp")
        softe = sem("softe")
        w_hi, w_lo = sem("w_hi"), sem("w_lo")
        exin_hi, exin_lo = sem("exin_hi"), sem("exin_lo")
        exout_hi, exout_lo = sem("exout_hi"), sem("exout_lo")
        up_done, down_done = sem("up_done"), sem("down_done")
        hid_hi, hid_lo = sem("hid_hi"), sem("hid_lo")
        sum_taken = sem("sum_taken")
        silu_done, gated_done = sem("silu_done"), sem("gated_done")
        gate_up, gate_prod, gate_logits = sem("gate_up"), sem("gate_prod"), sem("gate_logits")
        gate_shift, gate_exp = sem("gate_shift"), sem("gate_exp")
        x_mixed, x_hi, x_lo = sem("x_mixed"), sem("x_hi_done"), sem("x_lo_done")
        chain = sem("dve_chain")
        small_full = sem("small_full")
        x2_hi, x2_lo = sem("x2_hi"), sem("x2_lo")
        l2_up, l2_hid, l2_down = sem("l2_up"), sem("l2_hid"), sem("l2_down")
        y_done, mean_done, sq_done, var_done = sem("y_done"), sem("mean_done"), sem("sq_done"), sem("var_done")
        var_eps, rstd_done, diag_done, rstd_bc = sem("var_eps"), sem("rstd_done"), sem("diag_done"), sem("rstd_bc")
        z_done, z_scaled, x3_done = sem("z_done"), sem("z_scaled"), sem("x3_done")
        x3_hi, x3_lo, l3_done = sem("x3_hi"), sem("x3_lo"), sem("l3_done")
        out_ready, stored = sem("out_ready"), [sem("stored0"), sem("stored1")]

        def gate_ps(tb):
            return sums[0 if isinstance(tb, int) and tb == NB else 1]

        block = ctx.enter_context(nc.Block())

        def raw_slot(key):
            return AT[key] % RAW

        def raw_fill(key):
            return 16 * (AT[key] // RAW + 1)

        SMALL = 6
        n_small2 = 2 * B + B

        @block.sync
        def _(sp):
            def chunk_free(key, more=0):
                c = AT[key] - RAW
                if c < 0:
                    return
                kind, n = STREAM[c]
                if kind == "plain":
                    sp.wait_ge(w_lo, n + 1 + more)
                else:
                    sp.wait_ge(exin_lo, n + 1 + more)
                    sp.wait_ge(exout_lo, n + 1 + more)

            def load_plain(o, src):
                key = ("plain", o)
                chunk_free(key)
                sp.dma_start(raw[:, raw_slot(key)], src).then_inc(raw_full[raw_slot(key)], 16)

            def load_x(tb, o):
                key = ("plain", o)
                chunk_free(key)
                s = raw_slot(key)
                sp.dma_start(raw[:, s].rearrange("p (d n) -> p d n", d=DT),
                             xT_d[:, :, tb * BLK:(tb + 1) * BLK]).then_inc(raw_full[s], 16)

            def load_expert(tb, q, t, fixed=None):
                base = q if fixed is None else q + EX_CH * fixed
                more = 0 if fixed is not None else EX_CH * (tb - 1)
                key = ("expert", base if fixed is not None else base + EX_CH)
                chunk_free(key, more)
                s = raw_slot(key)
                sp.dma_start(raw[:, s], ex_d[t * 4 + q % 4]).then_inc(raw_full[s], 16)

            def expert_types(tb):
                t = [sp.value_load(idx[0:1, 0, bass.ds(tb * 2 + i, 1)] if not isinstance(tb, int)
                                   else idx[0:1, 0, tb * 2 + i:tb * 2 + i + 1], min_val=0, max_val=2) for i in range(2)]
                return [t[0], t[0] + 1, t[1], t[1] + 1]

            sp.dma_start(idx[:, 0], types_row_d[0:1]).then_inc(idx_full, 16)
            sp.dma_start(idx[:, 1], types_row_d[1:2]).then_inc(idx_full, 16)
            sp.dma_start(idx[:, 2], types_row_d[2:3]).then_inc(idx_full, 16)
            t = None
            for kind, n in STREAM[:EX_CH + PLAIN0]:
                if kind == "expert":
                    if t is None:
                        sp.wait_ge(idx_full, 48)
                        t = expert_types(0)
                    load_expert(0, n, t[n // 4], fixed=0)
                elif n == 0 or n > 4 * NSH:
                    load_x(0 if n == 0 else n - 4 * NSH, n)
                else:
                    load_plain(n, sh_d[n - 1])
            with sp.Fori(1, NB - 1) as tb:
                t = expert_types(tb)
                for q in range(EX_CH):
                    load_expert(tb, q, t[q // 4])
            t = expert_types(NB - 1)
            for kind, n in STREAM[AT[("expert", 48)]:AT[("expert", 63)] + 1]:
                if kind == "expert":
                    load_expert(NB - 1, n - 48, t[(n - 48) // 4], fixed=NB - 1)
                else:
                    load_plain(n, l1_d[n - PLAIN0])
            with sp.Fori(0, 4) as i:
                for r in range(12):
                    key = ("plain", PLAIN0 + 6 + r)
                    s = raw_slot(key)
                    if r < RAW:
                        sp.wait_ge(exin_lo, 64)
                        sp.wait_ge(exout_lo, 64)
                    sp.wait_ge(w_lo, PLAIN0 + 6 + r - 3 + i * 12)
                    sp.dma_start(raw[:, s], l1_d[i * 12 + 6 + r]).then_inc(raw_full[s], 16)
            langs = [sp.value_load(idx[0:1, 1, b:b + 1], min_val=0, max_val=w1_d.shape[0] - 1) for b in range(B)]
            subjs = [sp.value_load(idx[0:1, 2, b:b + 1], min_val=0, max_val=w3_d.shape[0] - 1) for b in range(B)]
            sp.wait_ge(x_mixed, NB)
            for b in range(B):
                key = ("plain", PLAIN0 + 6 * NE1 + b)
                chunk_free(key)
                s = raw_slot(key)
                sp.dma_start(raw[:, s, 0:512], w3_d[subjs[b]]).then_inc(raw_full[s], 16)
                sp.dma_start(raw[:, s, 512:640], w1_d[langs[b]]).then_inc(raw_full[s], 16)
                sp.dma_start(raw[0:A2, s, 640:896], w2_d[langs[b]]).then_inc(raw_full[s], 16)
                sp.dma_start(cols[:, b], cols_d[langs[b]]).then_inc(small_full, 16)
                sp.dma_start(b1[:, b:b + 1], b1_d[langs[b]]).then_inc(small_full, 16)
                sp.dma_start(biasb[:, b], bias_d[subjs[b]].to_broadcast([P, D])).then_inc(small_full, 16)
            for tb in range(NB):
                sp.wait_ge(out_ready, tb + 1)
                sp.dma_start(out_d[tb * BLK:(tb + 1) * BLK].rearrange("(q p) n -> p q n", p=P),
                             ostage[:, tb % 2]).then_inc(stored[tb % 2], 16)
            sp.wait_ge(stored[0], 32)
            sp.wait_ge(stored[1], 32)

        @block.tensor
        def _(pe):
            def product(out, wh, wl, vh, vl, start, stop):
                pe.matmul(out, wh, vh, start=start, stop=False)
                pe.matmul(out, wh, vl, start=False, stop=False)
                return pe.matmul(out, wl, vh, start=False, stop=stop)

            def x_block(tb, dt, half, n, t):
                lo = tb * BLK + half * S
                sl = slice(lo, lo + n) if isinstance(tb, int) else bass.ds(lo, n)
                return t[:, dt, sl]

            def l0_up(tb, n, first):
                job, f = L0_JOBS[n // FT], n % FT
                step = tb * L0_STEPS + n
                if n == 0 and not first:
                    pe.wait_ge(w_lo, 1 + 4 * NSH + tb)
                if first and job[0] == "shared" and f % 4 == 0:
                    if n == 0:
                        pe.wait_ge(w_lo, 1)
                    pe.wait_ge(w_lo, 1 + 4 * job[1] + 2 * (f // 4) + 1)
                if not (first and n < 2):
                    pe.wait_ge(hid_lo, step - 1)
                if job[0] == "shared":
                    N, half = BLK, 0
                    wt = lambda hl, dt: W[:, 2 * job[1], hl, f * D + dt * P:f * D + (dt + 1) * P]
                else:
                    N, half = S, job[1] // 2
                    q = (FT * job[1] + f) // 2
                    if f % 2 == 0:
                        pe.wait_ge(exin_lo, q + 1 + tb * EX_CH)
                    wt = lambda hl, dt: exin[:, q % 2, hl, f % 2 * D + dt * P:f % 2 * D + (dt + 1) * P]
                out = up_ps[:, n % 2, 0:N]
                for dt in range(DT):
                    last = product(out, wt(0, dt), wt(1, dt), x_block(tb, dt, half, N, xh), x_block(tb, dt, half, N, xl),
                                   dt == 0, dt == DT - 1)
                last.then_inc(up_done, 1)

            def l0_down(tb, n, first, last_block):
                jj, f = n // FT, n % FT
                job = L0_JOBS[jj]
                step = tb * L0_STEPS + n
                pair = 0 if last_block and jj == NJ - 1 else SUMS[jj]
                pe.wait_ge(hid_lo, step + 1)
                if f == 0:
                    before = [i for i in range(jj) if SUMS[i] == SUMS[jj]]
                    if last_block and jj == NJ - 1:
                        before = [4]
                    if before:
                        pe.wait_ge(sum_taken, NJ * tb + before[-1] + 1)
                    elif not first:
                        back = [i for i in range(NJ) if SUMS[i] == SUMS[jj]][-1]
                        pe.wait_ge(sum_taken, NJ * tb - NJ + back + 1)
                    if jj == 1 and not first:
                        pe.wait_ge(gate_shift, tb)
                if job[0] == "shared":
                    N = BLK
                    if first and f % 4 == 0:
                        pe.wait_ge(w_lo, 1 + 4 * job[1] + 2 * (f // 4) + 2)
                    wt = lambda hl, dt: W[:, 2 * job[1] + 1, hl, f * D + dt * P:f * D + (dt + 1) * P]
                else:
                    N = S
                    q = (FT * job[1] + f) // 2
                    if f % 2 == 0:
                        pe.wait_ge(exout_lo, q + 1 + tb * EX_CH)
                    wt = lambda hl, dt: exout[:, q % 2, hl, f % 2 * D + dt * P:f % 2 * D + (dt + 1) * P]
                for dt in range(DT):
                    last = product(sums[pair][:, dt, 0:N], wt(0, dt), wt(1, dt), hid[:, n % 2, 0, 0:N], hid[:, n % 2, 1, 0:N],
                                   f == 0, f == FT - 1)
                last.then_inc(down_done, 1)

            def gate_first(tb):
                pe.wait_ge(sum_taken, tb * NJ)
                prev = (tb - 1) * BLK
                for m in range(2):
                    for k in range(8):
                        w, dt = k // DT, k % DT
                        if w == 0:
                            row0 = x[:, dt, prev:prev + BLK:S] if isinstance(tb, int) else x[:, dt, bass.ds(prev, 2, S)]
                        else:
                            row0 = acc[:, w - 1, dt, 0:BLK:S]
                        last = pe.matmul(gate_ps(tb)[:, 0, 2 * m:2 * m + 2], gw1[:, k, m * P:(m + 1) * P], row0,
                                         start=k == 0, stop=k == 7)
                last.then_inc(gate_up, 1)

            def gate_second(tb):
                pe.wait_ge(gate_prod, tb)
                for m in range(2):
                    last = pe.matmul(gate_ps(tb)[:, 1, 0:8], ones[:], gprod[:, m].rearrange("p b c -> p (b c)"),
                                     start=m == 0, stop=m == 1)
                last.then_inc(gate_logits, 1)

            def l0_block(tb, first=False, last_block=False):
                for n in range(L0_STEPS):
                    l0_up(tb, n, first)
                    if n >= 2:
                        l0_down(tb, n - 2, first, last_block)
                    elif not first:
                        l0_down(tb - 1, L0_STEPS + n - 2, first, False)
                    if not first and n == 2:
                        gate_first(tb)
                    if not first and n == 4:
                        gate_second(tb)

            def l1_up(e, par, tb, f, loop=None):
                t = e * 32 + tb * FT + f
                if isinstance(e, int) and t < 2:
                    pe.wait_ge(hid_lo, L0_ALL + t - 1)
                else:
                    pe.wait_ge(gated_done, t - 1)
                if tb == 0 and f % 4 == 0:
                    pe.wait_ge(w_lo, PLAIN0 + 6 * e + 3 * (f // 4) + 2)
                if isinstance(e, int) and e == 0 and f == 0:
                    pe.wait_ge(x_lo, tb + 1)
                for m, ps in enumerate((up_ps, up2_ps)):
                    for dt in range(DT):
                        c = slice(f * D + dt * P, f * D + (dt + 1) * P)
                        last = product(ps[:, f % 2, :], W[:, 3 * par + m, 0, c], W[:, 3 * par + m, 1, c],
                                       xh[:, dt, tb * BLK:(tb + 1) * BLK], xl[:, dt, tb * BLK:(tb + 1) * BLK],
                                       dt == 0, dt == DT - 1)
                last.then_inc(up_done, 1)

            def l1_down(e, par, tb, f):
                pe.wait_ge(hid_lo, L0_ALL + e * 32 + tb * FT + f + 1)
                if f == 0:
                    pe.wait_ge(sum_taken, NB * NJ + 4 * e + tb)
                if tb == 0 and f % 4 == 0:
                    pe.wait_ge(w_lo, PLAIN0 + 6 * e + 3 * (f // 4) + 3)
                for dt in range(DT):
                    c = slice(f * D + dt * P, f * D + (dt + 1) * P)
                    last = product(sums[1][:, dt, :], W[:, 3 * par + 2, 0, c], W[:, 3 * par + 2, 1, c],
                                   hid[:, f % 2, 0, :], hid[:, f % 2, 1, :], f == 0, f == FT - 1)
                last.then_inc(down_done, 1)

            def l1_expert(e, par, first=False, hooks={}):
                for n in range(4 * FT):
                    l1_up(e, par, n // FT, n % FT)
                    if n >= 2:
                        l1_down(e, par, (n - 2) // FT, (n - 2) % FT)
                    elif not first:
                        l1_down(e - 1, 1 - par, 3, FT + n - 2)
                    else:
                        l0_down(NB - 1, L0_STEPS + n - 2, False, True)
                    if first and n == 2:
                        gate_first(NB)
                    if first and n == 4:
                        gate_second(NB)
                    for h in hooks.get(n, []):
                        h()

            def l2_first(tb):
                pe.wait_ge(x2_lo, tb + 1)
                pe.wait_ge(w_lo, PLAIN0 + 6 * NE1 + 2 * tb + 2)
                if tb:
                    pe.wait_ge(out_ready, tb)
                else:
                    pe.wait_ge(sum_taken, NB * NJ)
                for h in range(2):
                    b = 2 * tb + h
                    for dt in range(DT):
                        c = slice(dt * A2, (dt + 1) * A2)
                        t = slice(tb * BLK + h * S, tb * BLK + (h + 1) * S)
                        last = product(sums[0][0:A2, 0, h * S:(h + 1) * S], w1r[:, b, 0, c], w1r[:, b, 1, c],
                                       xh[:, dt, t], xl[:, dt, t], dt == 0, dt == DT - 1)
                last.then_inc(l2_up, 1)

            def l2_second(tb):
                pe.wait_ge(l2_hid, tb + 1)
                for h in range(2):
                    b = 2 * tb + h
                    for dt in range(DT):
                        c, t = slice(dt * P, (dt + 1) * P), slice(h * S, (h + 1) * S)
                        last = product(sums[0][:, dt, t], w2[:, b, 0, c], w2[:, b, 1, c], u[:, 0, t], u[:, 1, t], True, True)
                last.then_inc(l2_down, 1)

            def l2_mean(tb):
                pe.wait_ge(y_done, tb + 1)
                for dt in range(DT):
                    last = pe.matmul(sums[0][:, 0, :], ones[:], y[:, dt, :], start=dt == 0, stop=dt == DT - 1)
                last.then_inc(mean_done, 1)

            def l2_var(tb):
                pe.wait_ge(sq_done, tb + 1)
                for q in range(4):
                    for dt in range(DT):
                        last = pe.matmul(sums[0][:, 1, q:q + 1], sq[:, dt, q * P:(q + 1) * P], ones[:, 0:1],
                                         start=dt == 0, stop=dt == DT - 1)
                last.then_inc(var_done, 1)

            def l2_rstd(tb):
                pe.wait_ge(diag_done, tb + 1)
                last = pe.matmul(sums[0][:, 1, :], ones[:], diag[:].rearrange("p q n -> p (q n)"), start=True, stop=True)
                last.then_inc(rstd_bc, 1)

            def l3(tb):
                pe.wait_ge(x3_lo, tb + 1)
                for q in range(4):
                    b = 2 * tb + q // 2
                    t = slice(tb * BLK + q * P, tb * BLK + (q + 1) * P)
                    out = sums[0][:, q // 2, q % 2 * D:(q % 2 + 1) * D]
                    for dt in range(DT):
                        c = slice(dt * D, (dt + 1) * D)
                        pe.matmul(out, xh[:, dt, t], w3[:, b, 0, c], start=dt == 0, stop=False)
                        pe.matmul(out, xh[:, dt, t], w3[:, b, 1, c], start=False, stop=False)
                        pe.matmul(out[:, dt * P:(dt + 1) * P], xh[:, dt, t], identr[:], start=False, stop=False,
                                  skip_group_check=True)
                        pe.matmul(out[:, dt * P:(dt + 1) * P], xl[:, dt, t], identr[:], start=False, stop=False,
                                  skip_group_check=True)
                        last = pe.matmul(out, xl[:, dt, t], w3[:, b, 0, c], start=False, stop=dt == DT - 1)
                last.then_inc(l3_done, 1)

            l0_block(0, first=True)
            pe.wait_ge(consts, 1)
            pe.wait_ge(gw1_full, 16)
            with pe.Fori(1, NB - 1) as tb:
                l0_block(tb)
            l0_block(NB - 1, last_block=True)
            l1_expert(0, 0, first=True)
            l1_expert(1, 1)
            with pe.Fori(1, 4) as i:
                l1_expert(i * 2, 0)
                l1_expert(i * 2 + 1, 1)
            post = [l2_first, l2_second, l2_mean, l2_var, l2_rstd, l3]
            at = [3, 4, 5, 6, 7, 10]
            hooks = {}
            for tb in range(NB - 1):
                for stage, n in zip(post, at):
                    if 8 * (tb + 1) + n < 32:
                        hooks.setdefault(8 * (tb + 1) + n, []).append(lambda s=stage, tb=tb: s(tb))
            l1_expert(8, 0, hooks=hooks)
            l1_down(8, 0, 3, FT - 2)
            l1_down(8, 0, 3, FT - 1)
            l3(NB - 2)
            for stage in post:
                stage(NB - 1)

        @block.scalar
        def _(act):
            A = nc.scalar.activation

            def plain_hi(o, dst, more=0, fills=0):
                key = ("plain", o)
                act.wait_ge(raw_full[raw_slot(key)], raw_fill(key) + fills)
                src = raw[:, raw_slot(key)]
                if len(dst.shape) == 3:
                    src = src.rearrange("p (d n) -> p d n", d=DT)
                A(dst, src, ACT.Copy).then_inc(w_hi, 1)

            def shared_hi(o):
                j, r = (o - 1) // 4, (o - 1) % 4
                plain_hi(o, W[:, 2 * j + r % 2, 0, r // 2 * CH:(r // 2 + 1) * CH])

            def x_hi0(o):
                tb = 0 if o == 0 else o - 4 * NSH
                plain_hi(o, xh[:, :, tb * BLK:(tb + 1) * BLK])

            def expert_hi(ring, part, s, q, tb, loop):
                qq = q if loop else q + EX_CH * tb
                key = ("expert", qq + EX_CH if loop else qq)
                fills = 16 * (EX_CH // RAW) * (tb - 1) if loop else 0
                act.wait_ge(raw_full[raw_slot(key)], raw_fill(key) + fills)
                A(ring[:, q % 2, 0], raw[:, raw_slot(key), part * 512:(part + 1) * 512], ACT.Copy).then_inc(s, 1)

            def exout_hook(m, tb, loop):
                if m > 0:
                    act.wait_ge(down_done, L0_STEPS * tb + local_step(2 * m - 1) + 1)
                elif not (isinstance(tb, int) and tb == 0):
                    act.wait_ge(down_done, L0_STEPS * tb)
                expert_hi(exout, 1, exout_hi, m + 1, tb, loop)

            def mixed_hi(tb):
                act.wait_ge(x_mixed, tb)
                p = (tb - 1) * BLK
                sl = slice(p, p + BLK) if isinstance(tb, int) else bass.ds(p, BLK)
                A(xh[:, :, sl], x[:, :, sl], ACT.Copy).then_inc(x_hi, 1)

            def gate_exps(tb):
                act.wait_ge(gate_shift, tb)
                A(gexp[:].rearrange("p b c -> p (b c)"), gexp[:].rearrange("p b c -> p (b c)"), ACT.Exp).then_inc(gate_exp, 1)

            def l0_block(tb, hooks, first=False, last_block=False):
                loop = not isinstance(tb, int)
                for n in range(L0_STEPS):
                    kind, j = L0_JOBS[n // FT]
                    N = BLK if kind == "shared" else S
                    step = L0_STEPS * tb + n
                    act.wait_ge(up_done, step + 1)
                    if not (first and n < 2):
                        act.wait_ge(down_done, step - 1)
                    A(hid[:, n % 2, 0, 0:N], up_ps[:, n % 2, 0:N], ACT.Relu).then_inc(hid_hi, 1)
                    k = FT * j + n % FT
                    if kind == "expert" and k % 2 == 1:
                        m = k // 2
                        if not (last_block and m >= EX_CH - 2):
                            expert_hi(exin, 0, exin_hi, m + 2, tb, loop)
                        if not early_exout(m, first, last_block):
                            exout_hook(m, tb, loop)
                    if not first and n == 6:
                        gate_exps(tb)
                    if not first and n == FT:
                        mixed_hi(tb)
                    for h in hooks.get(n, []):
                        h()

            for dst, src in ((types, types_d), (gvec, gvec_d), (sg, sgate_d), (prob, prob_d), (gw2, gw2_d), (ident, ident_d)):
                act.dma_start(dst[:], src).then_inc(const_full, 16)
            act.wait_ge(softp, 1)
            A(gp[:], gp[:], ACT.Exp, scale=10.0).then_inc(softe, 1)
            act.dma_start(gw1[:], gw1_d).then_inc(gw1_full, 16)
            x_hi0(0)
            shared_hi(1)
            hooks = {n: [lambda o=n + 2: shared_hi(o)] for n in range(6)}
            hooks[6] = [lambda: expert_hi(exin, 0, exin_hi, 0, 0, False), lambda: expert_hi(exout, 1, exout_hi, 0, 0, False)]
            hooks[7] = [lambda: expert_hi(exin, 0, exin_hi, 1, 0, False)]
            for i in range(5):
                hooks[16 + i] = [lambda i=i: shared_hi(8 + i)]
            hooks[18].insert(0, lambda: exout_hook(4, 0, False))
            for i in range(3):
                hooks[21 + i] = [lambda i=i: x_hi0(13 + i)]
            l0_block(0, hooks, first=True)
            with act.Fori(1, NB - 1) as tb:
                l0_block(tb, {})

            def l1_weights_hi(e, r, par, more=0, fills=0):
                plain_hi(PLAIN0 + 6 * e + r, W[:, 3 * par + r % 3, 0, r // 3 * CH:(r // 3 + 1) * CH], more, fills)

            hooks = {FT * 4 + 2 + r: [lambda r=r: l1_weights_hi(0, r, 0)] for r in range(6)}
            hooks[FT * 4 + 2].insert(0, lambda: exout_hook(8, NB - 1, False))
            l0_block(NB - 1, hooks, last_block=True)

            def l1_expert(e, hooks, first=False):
                for n in range(4 * FT):
                    f = n % FT
                    t = e * 32 + n
                    start = first and n < 2
                    act.wait_ge(up_done, L0_ALL + t + 1)
                    if not start:
                        act.wait_ge(gated_done, t - 1)
                    A(sil[:, f % 2], up_ps[:, f % 2], ACT.Silu).then_inc(silu_done, 1)
                    act.wait_ge(gated_done, t + 1)
                    act.wait_ge(down_done, L0_ALL + t - 1)
                    A(hid[:, f % 2, 0], gat[:, f % 2], ACT.Copy).then_inc(hid_hi, 1)
                    if first and n == 6:
                        gate_exps(NB)
                    if first and n == FT:
                        mixed_hi(NB)
                    for h in hooks.get(n, []):
                        h()

            def next_weights(e, par, base, i):
                return {4 * (r + 1): [lambda r=r: l1_weights_hi(base + 1, r, 1 - par, 0, 0 if i is None else 48 * (i - 1))]
                        for r in range(6)}

            l1_expert(0, next_weights(0, 0, 0, None), first=True)
            l1_expert(1, next_weights(1, 1, 1, None))
            with act.Fori(1, 4) as i:
                l1_expert(i * 2, next_weights(None, 0, 2, i))
                l1_expert(i * 2 + 1, next_weights(None, 1, 3, i))

            def late_hi(b):
                key = ("plain", PLAIN0 + 6 * NE1 + b)
                s = raw_slot(key)
                before = sum(1 for bb in range(b) if raw_slot(("plain", PLAIN0 + 6 * NE1 + bb)) == s)
                act.wait_ge(raw_full[s], raw_fill(key) + 32 * (before + 1))
                A(w3[:, b, 0], raw[:, s, 0:512], ACT.Copy)
                A(w1r[:, b, 0], raw[:, s, 512:640], ACT.Copy)
                A(w2[:, b, 0], raw[0:A2, s, 640:896], ACT.Copy).then_inc(w_hi, 1)

            def x2_hi_part(tb):
                act.wait_ge(sum_taken, NB * NJ + 32 + tb + 1)
                sl = slice(tb * BLK, (tb + 1) * BLK)
                A(xh[:, :, sl], x[:, :, sl], ACT.Copy).then_inc(x2_hi, 1)

            def scale_z(tb):
                act.wait_ge(z_done, tb + 1)
                for dt in range(DT):
                    for h in range(2):
                        t = slice(h * S, (h + 1) * S)
                        last = A(y[:, dt, t], y[:, dt, t], ACT.Identity, bias=cols[:, 2 * tb + h, 4 + dt:5 + dt],
                                 scale=cols[:, 2 * tb + h, 2 + dt:3 + dt])
                last.then_inc(z_scaled, 1)

            def x3_hi_part(tb):
                act.wait_ge(x3_done, tb + 1)
                sl = slice(tb * BLK, (tb + 1) * BLK)
                A(xh[:, :, sl], x[:, :, sl], ACT.Copy).then_inc(x3_hi, 1)

            hooks = {2 + b: [lambda b=b: late_hi(b)] for b in range(B)}
            hooks[11] = [lambda: act.wait_ge(small_full, 16 * n_small2)]
            for tb in range(NB - 1):
                for stage, n in ((x2_hi_part, 2), (scale_z, 8), (x3_hi_part, 9)):
                    at = 8 * (tb + 1) + n
                    if at < 32:
                        hooks.setdefault(at, []).append(lambda s=stage, tb=tb: s(tb))
            l1_expert(8, hooks)
            scale_z(NB - 2)
            x3_hi_part(NB - 2)
            x2_hi_part(NB - 1)
            scale_z(NB - 1)
            x3_hi_part(NB - 1)

        @block.gpsimd
        def _(pool):
            def lo_part(dst, src, hi):
                return nc.gpsimd.tensor_tensor(dst, src, hi.bitcast(f32), ALU.subtract)

            def plain_lo(o, dst, hi, more=0):
                key = ("plain", o)
                pool.wait_ge(w_hi, o + 1 + more)
                src = raw[:, raw_slot(key)]
                if len(dst.shape) == 3:
                    src = src.rearrange("p (d n) -> p d n", d=DT)
                lo_part(dst, src, hi).then_inc(w_lo, 1)

            def shared_or_x_lo(o):
                if o == 0 or o > 4 * NSH:
                    tb = 0 if o == 0 else o - 4 * NSH
                    sl = slice(tb * BLK, (tb + 1) * BLK)
                    plain_lo(o, xl[:, :, sl], xh[:, :, sl])
                else:
                    j, r = (o - 1) // 4, (o - 1) % 4
                    c = slice(r // 2 * CH, (r // 2 + 1) * CH)
                    plain_lo(o, W[:, 2 * j + r % 2, 1, c], W[:, 2 * j + r % 2, 0, c])

            def expert_lo(q, tb, loop):
                qq = q + EX_CH if loop else q + EX_CH * tb
                s = raw_slot(("expert", qq))
                pool.wait_ge(exin_hi, q + EX_CH * tb + 1)
                lo_part(exin[:, q % 2, 1], raw[:, s, 0:512], exin[:, q % 2, 0]).then_inc(exin_lo, 1)

            def mixed_lo(tb):
                pool.wait_ge(x_hi, tb)
                p = (tb - 1) * BLK
                sl = slice(p, p + BLK) if isinstance(tb, int) else bass.ds(p, BLK)
                lo_part(xl[:, :, sl], x[:, :, sl], xh[:, :, sl]).then_inc(x_lo, 1)

            def l1_lo(e, r, par, more=0):
                c = slice(r // 3 * CH, (r // 3 + 1) * CH)
                plain_lo(PLAIN0 + 6 * e + r, W[:, 3 * par + r % 3, 1, c], W[:, 3 * par + r % 3, 0, c], more)

            for kind, n in STREAM[:AT[("expert", 17)] + 1]:
                if kind == "plain":
                    shared_or_x_lo(n)
                else:
                    expert_lo(n, 0, False)
            with pool.Fori(1, NB - 1) as tb:
                mixed_lo(tb)
                for q in range(2, EX_CH + 2):
                    expert_lo(q, tb, True)
            mixed_lo(NB - 1)
            for kind, n in STREAM[AT[("expert", 50)]:AT[("expert", 63)] + 1]:
                if kind == "plain":
                    l1_lo(0, n - PLAIN0, 0)
                else:
                    expert_lo(n - 48, NB - 1, False)

            l1_lo(1, 0, 1)
            mixed_lo(NB)
            for r in range(1, 6):
                l1_lo(1, r, 1)
            for r in range(6):
                l1_lo(2, r, 0)
            with pool.Fori(1, 4) as i:
                for e, par in ((3, 1), (4, 0)):
                    for r in range(6):
                        l1_lo(e, r, par, (i - 1) * 12)

            def late_lo(b):
                o = PLAIN0 + 6 * NE1 + b
                s = raw_slot(("plain", o))
                pool.wait_ge(w_hi, o + 1)
                lo_part(w3[:, b, 1], raw[:, s, 0:512], w3[:, b, 0])
                lo_part(w1r[:, b, 1], raw[:, s, 512:640], w1r[:, b, 0])
                lo_part(w2[:, b, 1], raw[0:A2, s, 640:896], w2[:, b, 0]).then_inc(w_lo, 1)

            def block_lo(ready, done, tb):
                pool.wait_ge(ready, tb + 1)
                sl = slice(tb * BLK, (tb + 1) * BLK)
                lo_part(xl[:, :, sl], x[:, :, sl], xh[:, :, sl]).then_inc(done, 1)

            def rstd_pow(tb):
                pool.wait_ge(var_eps, tb + 1)
                nc.gpsimd.tensor_tensor(rstd[:], var[:], mhalf[:], ALU.pow).then_inc(rstd_done, 1)

            for b in range(B):
                late_lo(b)
            pool.wait_ge(consts, 1)
            order = sorted([(8 * tb + n, tb, k) for tb in range(NB) for k, n in ((0, 2), (1, 6), (2, 9))])
            for _, tb, k in order:
                if k == 0:
                    block_lo(x2_hi, x2_lo, tb)
                elif k == 1:
                    rstd_pow(tb)
                else:
                    block_lo(x3_hi, x3_lo, tb)

        @block.vector
        def _(dve):
            V = nc.vector
            n_chain = [0]

            def linked(ins):
                ins.then_inc(chain, 1)
                n_chain[0] = n_chain[0] + 1
                dve.wait_ge(chain, n_chain[0])

            V.memset(ones[:], 1.0)
            V.memset(mhalf[:], -0.5)
            dve.wait_ge(const_full, 16 * SMALL)
            V.tensor_copy(identr[:], ident[:])
            V.tensor_copy(typesf[:], types[:])
            linked(V.tensor_reduce(gmax[:], gvec[:], AX.X, ALU.max))
            V.tensor_tensor(gp[:], gvec[:], gmax[:].rearrange("p (t o) -> p t o", o=1).to_broadcast([P, 3, 4]),
                            ALU.subtract).then_inc(softp, 1)
            linked(V.tensor_scalar(omg[:], sg[:], -1.0, 1.0, ALU.mult, ALU.add))
            V.tensor_tensor(coef[:, 0:NE1 - 1, :], prob[:].rearrange("p b e -> p e b"),
                            omg[:].rearrange("p (o b) -> p o b", o=1).to_broadcast([P, NE1 - 1, B]), ALU.mult)
            V.tensor_copy(coef[:, NE1 - 1, :], sg[:]).then_inc(consts, 1)
            dve.wait_ge(softe, 1)
            linked(V.tensor_reduce(gmax[:], gp[:], AX.X, ALU.add))
            linked(V.reciprocal(gmax[:], gmax[:]))
            linked(V.tensor_tensor(gp[:], gp[:], gmax[:].rearrange("p (t o) -> p t o", o=1).to_broadcast([P, 3, 4]),
                                   ALU.mult))
            for t in range(3):
                dst = wab if t == 0 else wtmp
                for s in range(2):
                    last = V.tensor_scalar(dst[:, s], typesf[:], float(t), gp[:, t, t + s:t + s + 1],
                                           ALU.is_equal, ALU.mult)
                linked(last)
                if t:
                    linked(V.tensor_tensor(wab[:], wab[:], wtmp[:], ALU.add))

            def l0_take(tb, jj, last_block):
                kind, j = L0_JOBS[jj]
                pair = sums[0 if last_block and jj == NJ - 1 else SUMS[jj]]
                dve.wait_ge(down_done, L0_STEPS * tb + FT * (jj + 1))
                if kind == "shared":
                    V.tensor_copy(acc[:, j], pair[:]).then_inc(sum_taken, 1)
                    return
                b, s = j // 2, j % 2
                if s == 1:
                    dve.wait_ge(sum_taken, NJ * tb + jj)
                p = tb * BLK + b * S
                dyn = not isinstance(tb, int)
                ex = x[:, :, bass.ds(p, S)] if dyn else x[:, :, p:p + S]
                w = wab[:, s, bass.ds(tb * 2 + b, 1)] if dyn else wab[:, s, 2 * tb + b:2 * tb + b + 1]
                if s == 0:
                    V.tensor_scalar(ex, pair[:, :, 0:S], w, None, ALU.mult).then_inc(sum_taken, 1)
                else:
                    V.scalar_tensor_tensor(ex, pair[:, :, 0:S], w, ex, ALU.mult, ALU.add).then_inc(sum_taken, 1)

            def gate_hidden(tb):
                dve.wait_ge(gate_up, tb)
                linked(V.tensor_scalar(r1[:].rearrange("p m b -> p (m b)"), gate_ps(tb)[:, 0, 0:4], 0.0, None, ALU.max))
                for m in range(2):
                    for b in range(2):
                        last = V.tensor_scalar(gprod[:, m, b], gw2[:, m], r1[:, m, b:b + 1], None, ALU.mult)
                last.then_inc(gate_prod, 1)

            def gate_shifted(tb):
                dve.wait_ge(gate_logits, tb)
                lg = gate_ps(tb)[:, 1, 0:8].rearrange("p (b c) -> p b c", b=2)
                linked(V.tensor_reduce(glmax[:], lg, AX.X, ALU.max))
                V.tensor_tensor(gexp[:], lg, glmax[:].rearrange("p (b o) -> p b o", o=1).to_broadcast([P, 2, 4]),
                                ALU.subtract).then_inc(gate_shift, 1)

            def gate_probs(tb):
                dve.wait_ge(gate_exp, tb)
                linked(V.tensor_reduce(gsum[:], gexp[:], AX.X, ALU.add))
                linked(V.reciprocal(gsum[:], gsum[:]))
                linked(V.tensor_tensor(g[:], gexp[:], gsum[:].rearrange("p (b o) -> p b o", o=1).to_broadcast([P, 2, 4]),
                                       ALU.mult))

            def mix(tb, b):
                p = (tb - 1) * BLK + b * S
                sl = slice(p, p + S) if isinstance(tb, int) else bass.ds(p, S)
                xb = x[:, :, sl]
                linked(V.scalar_tensor_tensor(xb, xb, g[:, b, 0:1], xh[:, :, sl].bitcast(f32), ALU.mult, ALU.add))
                linked(V.tensor_tensor(xb, xb, xl[:, :, sl].bitcast(f32), ALU.add))
                for j in range(NSH):
                    ins = V.scalar_tensor_tensor(xb, acc[:, j, :, b * S:(b + 1) * S], g[:, b, j + 1:j + 2], xb,
                                                 ALU.mult, ALU.add)
                    if j < NSH - 1:
                        linked(ins)
                if b == 1:
                    ins.then_inc(x_mixed, 1)

            def gate_hooks(tb, n):
                if n == 3:
                    gate_hidden(tb)
                if n == 5:
                    gate_shifted(tb)
                if n == 6:
                    gate_probs(tb)
                    mix(tb, 0)
                if n == 7:
                    mix(tb, 1)

            CHAIN_GATE = 1 + 1 + 3 + 8

            def l0_block(tb, first=False, last_block=False):
                loop = not isinstance(tb, int)
                for n in range(L0_STEPS):
                    jj = n // FT
                    kind, j = L0_JOBS[jj]
                    N = BLK if kind == "shared" else S
                    dve.wait_ge(hid_hi, L0_STEPS * tb + n + 1)
                    V.scalar_tensor_tensor(hid[:, n % 2, 1, 0:N], up_ps[:, n % 2, 0:N], 0.0,
                                           hid[:, n % 2, 0, 0:N].bitcast(f32), ALU.max, ALU.subtract).then_inc(hid_lo, 1)
                    if n % FT == 1:
                        if jj:
                            l0_take(tb, jj - 1, last_block)
                        elif not first:
                            l0_take(tb - 1, NJ - 1, False)
                    if not first and n < FT:
                        gate_hooks(tb, n)
                    k = FT * j + n % FT
                    if kind == "expert" and k % 2 == 1 and not early_exout(k // 2, first, last_block):
                        expert_lo(k // 2 + 1, tb, loop)
                    if first and n == 6:
                        expert_lo(0, 0, False)
                    if first and n == 18:
                        expert_lo(5, 0, False)
                    if last_block and n == 34:
                        expert_lo(9, tb, False)

            def expert_lo(q, tb, loop):
                qq = q + EX_CH if loop else q + EX_CH * tb
                s = raw_slot(("expert", qq))
                dve.wait_ge(exout_hi, q + EX_CH * tb + 1)
                V.tensor_tensor(exout[:, q % 2, 1], raw[:, s, 512:1024], exout[:, q % 2, 0].bitcast(f32),
                                ALU.subtract).then_inc(exout_lo, 1)

            l0_block(0, first=True)
            c0 = n_chain[0]
            with dve.Fori(1, NB - 1) as tb:
                n_chain[0] = tb * CHAIN_GATE + (c0 - CHAIN_GATE)
                l0_block(tb)
            n_chain[0] = c0 + 2 * CHAIN_GATE
            l0_block(NB - 1, last_block=True)

            def l1_take(e, tb):
                dve.wait_ge(down_done, L0_ALL + 32 * e + FT * (tb + 1))
                for b in range(2):
                    t = slice(tb * BLK + b * S, tb * BLK + (b + 1) * S)
                    bb = 2 * tb + b
                    w = coef[:, e, bb:bb + 1] if isinstance(e, int) else coef[:, bass.ds(e, 1), bb]
                    last = V.scalar_tensor_tensor(x[:, :, t], sums[1][:, :, b * S:(b + 1) * S], w, x[:, :, t],
                                                  ALU.mult, ALU.add)
                last.then_inc(sum_taken, 1)

            def l1_expert(e, first=False, hooks={}):
                for n in range(4 * FT):
                    f = n % FT
                    t = e * 32 + n
                    dve.wait_ge(silu_done, t + 1)
                    V.tensor_tensor(gat[:, f % 2], up2_ps[:, f % 2], sil[:, f % 2], ALU.mult).then_inc(gated_done, 1)
                    dve.wait_ge(hid_hi, L0_ALL + t + 1)
                    V.tensor_tensor(hid[:, f % 2, 1], gat[:, f % 2], hid[:, f % 2, 0].bitcast(f32),
                                    ALU.subtract).then_inc(hid_lo, 1)
                    if f == 1:
                        if n > 1:
                            l1_take(e, n // FT - 1)
                        elif first:
                            l0_take(NB - 1, NJ - 1, True)
                        else:
                            l1_take(e - 1, 3)
                    if first and n < FT:
                        gate_hooks(NB, n)
                    for h in hooks.get(n, []):
                        h()

            l1_expert(0, first=True)
            l1_expert(1)
            with dve.Fori(1, 4) as i:
                l1_expert(i * 2)
                l1_expert(i * 2 + 1)

            def l2_hidden(tb):
                dve.wait_ge(l2_up, tb + 1)
                for h in range(2):
                    t = slice(h * S, (h + 1) * S)
                    last = V.tensor_scalar(ru[:, t], sums[0][0:A2, 0, t], b1[:, 2 * tb + h:2 * tb + h + 1], 0.0,
                                           ALU.add, ALU.max)
                linked(last)
                linked(V.tensor_copy(u[:, 0], ru[:]))
                V.tensor_tensor(u[:, 1], ru[:], u[:, 0].bitcast(f32), ALU.subtract).then_inc(l2_hid, 1)

            def l2_residual(tb):
                dve.wait_ge(l2_down, tb + 1)
                for dt in range(DT):
                    for h in range(2):
                        t = slice(h * S, (h + 1) * S)
                        last = V.scalar_tensor_tensor(y[:, dt, t], sums[0][:, dt, t], cols[:, 2 * tb + h, dt:dt + 1],
                                                      x[:, dt, tb * BLK + h * S:tb * BLK + (h + 1) * S], ALU.add, ALU.add)
                last.then_inc(y_done, 1)

            def l2_center(tb):
                dve.wait_ge(mean_done, tb + 1)
                for dt in range(DT):
                    last = V.scalar_tensor_tensor(y[:, dt], sums[0][:, 0], -1.0 / D, y[:, dt], ALU.mult, ALU.add)
                linked(last)
                V.tensor_tensor(sq[:], y[:], y[:], ALU.mult).then_inc(sq_done, 1)

            def l2_var_eps(tb):
                dve.wait_ge(var_done, tb + 1)
                V.tensor_scalar(var[:], sums[0][:, 1, 0:4], 1.0 / D, 1e-5, ALU.mult, ALU.add).then_inc(var_eps, 1)
                dve.wait_ge(rstd_done, tb + 1)
                for q in range(4):
                    last = V.tensor_scalar(diag[:, q], ident[:], rstd[:, q:q + 1], None, ALU.mult)
                last.then_inc(diag_done, 1)

            def l2_normed(tb):
                dve.wait_ge(rstd_bc, tb + 1)
                for dt in range(DT):
                    last = V.tensor_tensor(y[:, dt], sums[0][:, 1], y[:, dt], ALU.mult)
                last.then_inc(z_done, 1)

            def l2_out(tb):
                dve.wait_ge(z_scaled, tb + 1)
                xb = x[:, :, tb * BLK:(tb + 1) * BLK]
                V.tensor_tensor(xb, xb, y[:], ALU.add).then_inc(x3_done, 1)

            def l3_out(tb):
                dve.wait_ge(l3_done, tb + 1)
                if tb >= 2:
                    dve.wait_ge(stored[tb % 2], 16)
                for h in range(2):
                    last = V.tensor_tensor(ostage[:, tb % 2, 2 * h:2 * h + 2],
                                           sums[0][:, h].rearrange("p (q n) -> p q n", q=2),
                                           biasb[:, 2 * tb + h:2 * tb + h + 1].to_broadcast([P, 2, D]), ALU.add)
                last.then_inc(out_ready, 1)

            post = [(l2_hidden, 3), (l2_residual, 4), (l2_center, 5), (l2_var_eps, 6), (l2_normed, 7), (l2_out, 8),
                    (l3_out, 10)]
            hooks = {10: [lambda: dve.wait_ge(small_full, 16 * n_small2)]}
            for tb in range(NB - 1):
                for stage, n in post:
                    if 8 * (tb + 1) + n < 32:
                        hooks.setdefault(8 * (tb + 1) + n, []).append(lambda s=stage, tb=tb: s(tb))
            l1_expert(8, hooks=hooks)
            l2_out(NB - 2)
            l1_take(8, 3)
            l3_out(NB - 2)
            for stage, _ in post:
                stage(NB - 1)



def kernel(**inputs):
    import numpy as np
    import concourse.bacc as bacc
    from concourse import mybir
    from concourse.bass_utils import run_bass_kernel_spmd

    v = {k: np.asarray(a) for k, a in inputs.items()}

    def by_rows(w):
        n = w.shape[0]
        return w.reshape(n, DT, P, FT, P).transpose(0, 2, 3, 1, 4).reshape(n, P, FT * D)

    def by_hidden(w):
        n = w.shape[0]
        return w.reshape(n, FT, P, D).transpose(0, 2, 1, 3).reshape(n, P, FT * D)

    def chunks(mats):
        s = np.stack([m.reshape(m.shape[0], P, 2, CH) for m in mats], axis=1)
        return s.transpose(0, 3, 1, 2, 4).reshape(-1, P, CH)

    shared = chunks([by_rows(v["L0_cond_share_wi"]), by_hidden(v["L0_cond_share_wo"])])
    ei = by_rows(v["L0_cond_expert_wi"]).reshape(4, P, 4, 512)
    eo = by_hidden(v["L0_cond_expert_wo"]).reshape(4, P, 4, 512)
    experts = np.concatenate([ei, eo], axis=3).transpose(0, 2, 1, 3).reshape(16, P, CH)
    cat = lambda a, b: np.concatenate([v[a], v[b][None]], axis=0)
    l1 = chunks([by_rows(cat("L1_cond_Wg", "L1_cond_Sg")), by_rows(cat("L1_cond_Wu", "L1_cond_Su")),
                 by_hidden(cat("L1_cond_Wd", "L1_cond_Sd"))])
    col = lambda a: a.reshape(-1, DT, P).transpose(0, 2, 1)
    arrays = {
        "xT": v["x"].reshape(B * S, DT, P).transpose(2, 1, 0),
        "shared": shared, "experts": experts, "l1": l1,
        "types": np.broadcast_to(v["itok_B_0_2"], (P, B)),
        "types_row": np.stack([v["itok_B_0_2"], v["itok_B_0_8"], v["itok_B_0_7"]]),
        "gvec": np.broadcast_to(v["L0_cond_gate_vecs"], (P, 3, 4)),
        "gw1": v["L0_cond_gate_w1"].reshape(8, P, D).transpose(1, 0, 2),
        "gw2": v["L0_cond_gate_w2"].reshape(2, P, 4).transpose(1, 0, 2),
        "prob": np.broadcast_to(v["fside_Bx8_0"], (P, B, 8)),
        "sgate": np.broadcast_to(v["condB_sharedgateprob"], (P, B)),
        "w1": v["L2_cond_W1"].reshape(-1, DT, P, A2).transpose(0, 2, 1, 3).reshape(-1, P, DT * A2),
        "w2": v["L2_cond_W2"],
        "b1": v["L2_cond_b1"][:, :, None],
        "cols": np.concatenate([col(v["L2_cond_b2"]), col(v["L2_cond_gamma"]), col(v["L2_cond_beta"])], axis=2),
        "w3": v["L3_cond_weight"].transpose(0, 2, 1).reshape(-1, DT, P, D).transpose(0, 2, 1, 3).reshape(-1, P, DT * D),
        "bias": v["L3_cond_bias"][:, None, :],
        "ident": np.eye(P, dtype=np.float32),
    }
    arrays = {f"in_{k}": np.ascontiguousarray(a) for k, a in arrays.items()}
    nc = bacc.Bacc("TRN2", target_bir_lowering=False, num_devices=1)
    ap = {k[3:]: nc.dram_tensor(k, a.shape, mybir.dt.from_np(a.dtype), kind="ExternalInput").ap()
          for k, a in arrays.items()}
    out = nc.dram_tensor("out", (B * S, D), mybir.dt.float32, kind="ExternalOutput").ap()
    build(nc, ap["xT"], ap["shared"], ap["experts"], ap["l1"], ap["types"], ap["types_row"], ap["gvec"], ap["gw1"],
          ap["gw2"], ap["prob"], ap["sgate"], ap["w1"], ap["w2"], ap["b1"], ap["cols"], ap["w3"],
          ap["bias"], ap["ident"], out)
    r = run_bass_kernel_spmd(nc, [arrays], core_ids=[0])
    return r.results[0]["out"].reshape(B, S, D)
```

```python
import concourse.bass as bass
from concourse import mybir
from contextlib import ExitStack


B, S, D, F = 8, 256, 256, 1024
P = 128
DT = D // P
FT = F // P
NB = 4
BLK = B * S // NB
NSH = 3
NE1 = 9
A2 = 64
CH = 1024
RAW = 4
L0_JOBS = [("shared", 0), ("expert", 0), ("shared", 1), ("expert", 1), ("shared", 2), ("expert", 2), ("expert", 3)]
NJ = len(L0_JOBS)
L0_STEPS = NJ * FT
L0_ALL = NB * L0_STEPS
EX_STEPS = 4 * FT
EX_CH = EX_STEPS // 2
SUMS = [0, 1, 0, 1, 0, 1, 0]
PLAIN0 = 4 + 4 * NSH
LAST_JOBS = [(0, BLK), (BLK, BLK), (2 * BLK, BLK), (3 * BLK, S), (3 * BLK + S, S)]
L1_STEPS = 4 * FT
STAGES = ["x2", "up", "hid", "down", "res", "mean", "center", "scale", "var", "eps", "rstd", "norm", "x3", "l3", "out"]
WHEN = [dict(zip(STAGES, [base + n for n in at])) for base, at in (
    (8, (2, 3, 3, 4, 4, 5, 5, 6, 6, 6, 7, 7, 8, 9, 9)),
    (16, (2, 3, 3, 4, 4, 5, 5, 6, 6, 6, 7, 7, 8, 9, 9)),
    (24, (2, 4, 4, 6, 6, 7, 7, 8, 9, 9, 10, 10, 12, 13, 13)),
    (32, (2, 3, 3, 5, 5, 6, 6, 7, 7, 8, 9, 9, 10, 11, 11)),
    (40, (2, 3, 3, 4, 4, 5, 5, 6, 6, 6, 7, 7, 8, 9, 9)))]


def job_of_expert(j):
    return [i for i, (kind, n) in enumerate(L0_JOBS) if kind == "expert" and n == j][0]


def exout_at(k, first, last_block):
    q = (k + 1) // 2
    if k == 0 or (k % 2 == 1) != (q % 4 == 0):
        return None
    if first and q == 5 or last_block and q in (9, EX_CH):
        return None
    return q


def local_step(k):
    return FT * job_of_expert(k // FT) + k % FT


def stream_table():
    sh = lambda j, m, h: ("plain", 1 + 4 * j + 2 * h + m)
    t = [("plain", 0), sh(0, 0, 0), sh(0, 1, 0), sh(0, 0, 1), sh(0, 1, 1),
         sh(1, 0, 0), sh(1, 1, 0), sh(1, 0, 1), ("expert", 0), ("expert", 1), ("expert", 2), ("expert", 3), ("expert", 4), ("expert", 5),
         sh(1, 1, 1)] + [sh(2, m, h) for h in range(2) for m in range(2)]
    t += [("plain", 13), ("plain", 14), ("plain", 15)]
    t += [("expert", q) for q in range(6, 58)]
    t += [("plain", PLAIN0 + r) for r in range(6)]
    t += [("expert", q) for q in range(58, 64)]
    t += [("plain", PLAIN0 + r) for r in range(6, 6 * NE1 + B)]
    return t


STREAM = stream_table()
AT = {k: c for c, k in enumerate(STREAM)}


def build(nc, xT_d, sh_d, ex_d, l1_d, types_d, types_row_d, gvec_d, gw1_d, gw2_d, prob_d, sgate_d, w1_d, w2_d, b1_d, cols_d, w3_d, bias_d, ident_d, out_d):
    f32, f32r, i32 = mybir.dt.float32, mybir.dt.float32r, mybir.dt.int32
    ALU, ACT, AX = mybir.AluOpType, mybir.ActivationFunctionType, mybir.AxisListType

    size = {f32: 4, f32r: 4, i32: 4}
    top = [(nc.sbuf_base + 31) // 32 * 32]

    def place(name, shape, dt, over=None, skip=0):
        n = size[dt]
        for s in shape[1:]:
            n *= s
        if over is None:
            at = top[0]
            top[0] += (n + 31) // 32 * 32
        else:
            at = where[over] + skip
        where[name] = at
        return nc.alloc_sbuf_tensor_at(name, shape, dt, offset=at)

    where = {}
    W = place("weights", [P, 6, 2, FT * D], f32r)
    raw = place("raw", [P, RAW, CH], f32)
    exin = place("expert_in", [P, 2, 2, 512], f32r)
    exout = place("expert_out", [P, 2, 2, 512], f32r)
    x = place("x", [P, DT, B * S], f32)
    xh = place("x_hi", [P, DT, B * S], f32r)
    xl = place("x_lo", [P, DT, B * S], f32r)
    acc = place("shared_sums", [P, NSH, DT, BLK], f32)
    hid = place("hidden", [P, 2, 2, BLK], f32r)
    gw1 = place("gate_w1", [P, 8, D], f32)
    gw2 = place("gate_w2", [P, 2, 4], f32)
    ones = place("ones", [P, P], f32)
    types = place("types", [P, B], i32)
    typesf = place("types_f", [P, B], f32)
    idx = place("idx", [1, 3, B], i32)
    gvec = place("gate_vecs", [P, 3, 4], f32)
    gmax = place("gate_vec_max", [P, 3], f32)
    gp = place("gate_vec_probs", [P, 3, 4], f32)
    wab = place("expert_weight", [P, 2, B], f32)
    wtmp = place("expert_weight_part", [P, 2, B], f32)
    prob = place("prob", [P, B, NE1 - 1], f32)
    sg = place("shared_gate", [P, B], f32)
    omg = place("one_minus_gate", [P, B], f32)
    coef = place("l1_coef", [P, NE1, B], f32)
    r1 = place("gate_hidden", [P, 2, 2], f32)
    gpart = place("gate_partial", [P, 2, D], f32)
    gprod = place("gate_products", [P, 2, 2, 4], f32)
    glmax = place("gate_logit_max", [P, 2], f32)
    gexp = place("gate_exp", [P, 2, 4], f32)
    gsum = place("gate_sum", [P, 2], f32)
    g = place("gate", [P, 2, 4], f32)
    mhalf = place("minus_half", [P, 4], f32)
    assert top[0] <= nc.sbuf_usable_end, (top[0], nc.sbuf_usable_end)
    sil = place("silu", [P, 2, BLK], f32, over="expert_in")
    gat = place("gated", [P, 2, BLK], f32, over="expert_in", skip=4 * 2 * BLK)
    ostage = place("out_stage", [P, 2, 4, D], f32, over="expert_out")
    biasb = place("l3_bias", [P, B, D], f32, over="shared_sums")
    diag = place("rstd_diag", [P, 4, P], f32, over="shared_sums", skip=4 * B * D)
    ident = place("ident", [P, P], f32, over="shared_sums", skip=4 * B * D + 16 * P)
    identr = place("ident_r", [P, P], f32r, over="shared_sums", skip=4 * B * D + 20 * P)
    cols = place("l2_cols", [P, B, 6], f32, over="shared_sums", skip=4 * B * D + 24 * P)
    b1 = place("l2_b1", [A2, B], f32, over="shared_sums", skip=4 * B * D + 26 * P)
    var = place("variance", [P, 4], f32, over="shared_sums", skip=4 * B * D + 27 * P)
    rstd = place("rstd", [P, 4], f32, over="shared_sums", skip=4 * B * D + 28 * P)
    w1r = place("l2_w1", [P, B, 2, DT * A2], f32r, over="gate_w1")
    y = place("y", [P, DT, BLK], f32, over="raw")
    sq = place("squares", [P, DT, BLK], f32, over="raw", skip=4096)
    ru = place("l2_hidden", [A2, BLK], f32, over="raw", skip=8192)
    u = place("l2_hidden_r", [A2, 2, BLK], f32r, over="raw", skip=10240)
    w3 = W[:, 3:5].rearrange("p s h n -> p (s h n)").rearrange("p (b h n) -> p b h n", b=B, h=2)
    w2 = W[0:A2, 5].rearrange("p h n -> p (h n)").rearrange("p (b h n) -> p b h n", b=B, h=2)

    ctx = ExitStack()
    with ctx:
        def bank(name, n):
            return ctx.enter_context(nc.psum_tensor(name, [P, n, 512], f32))

        def sem(name):
            return ctx.enter_context(nc.semaphore(name))

        up_ps = bank("up", 4)
        sums = [bank("sum0", 2), bank("sum1", 2)]
        unit_ps = [sums[0], sums[0], sums[0], up_ps[:, 2:4], sums[0]]

        raw_full = [sem(f"raw_full{i}") for i in range(RAW)]
        const_full, gw1_full = sem("const_full"), sem("gw1_full")
        idx_full = sem("idx_full")
        consts = sem("consts")
        softp = sem("softp")
        softe = sem("softe")
        w_hi, w_lo = sem("w_hi"), sem("w_lo")
        exin_hi, exin_lo = sem("exin_hi"), sem("exin_lo")
        exout_hi, exout_lo = sem("exout_hi"), sem("exout_lo")
        up_done, down_done = sem("up_done"), sem("down_done")
        hid_hi, hid_lo = sem("hid_hi"), sem("hid_lo")
        sum_taken = sem("sum_taken")
        silu_done, gated_done = sem("silu_done"), sem("gated_done")
        gate_part, gate_up, gate_prod, gate_logits = sem("gate_part"), sem("gate_up"), sem("gate_prod"), sem("gate_logits")
        gate_shift, gate_exp = sem("gate_shift"), sem("gate_exp")
        x_mixed, x_hi, x_lo = sem("x_mixed"), sem("x_hi_done"), sem("x_lo_done")
        chain = sem("dve_chain")
        small_full = sem("small_full")
        x2_hi, x2_lo = sem("x2_hi"), sem("x2_lo")
        l2_up, l2_hid, l2_down = sem("l2_up"), sem("l2_hid"), sem("l2_down")
        y_done, mean_done, sq_done, var_done = sem("y_done"), sem("mean_done"), sem("sq_done"), sem("var_done")
        var_eps, rstd_done, diag_done, rstd_bc = sem("var_eps"), sem("rstd_done"), sem("diag_done"), sem("rstd_bc")
        y_scaled, x3_done = sem("y_scaled"), sem("x3_done")
        x3_hi, x3_lo, l3_done = sem("x3_hi"), sem("x3_lo"), sem("l3_done")
        out_ready, stored = sem("out_ready"), [sem("stored0"), sem("stored1")]

        def l1_sum(job, last_e):
            return sums[1 if last_e else (job + 1) % 2]

        def gate_ps(tb):
            return sums[0 if isinstance(tb, int) and tb == NB else 1]

        def ex_slot(n):
            return slice(n // 2 % 2 * S, (n // 2 % 2 + 1) * S)

        def last_steps(step, hooks):
            for T in range(40):
                job = T // FT
                step(T, *LAST_JOBS[job])
                for h in hooks.get(T, []):
                    h()

        def placed(stages):
            hooks = {}
            for name in STAGES:
                for u in range(len(WHEN)):
                    if name in stages:
                        hooks.setdefault(WHEN[u][name], []).append((u, STAGES.index(name), stages[name]))
            return {T: [lambda f=f, u=u: f(u) for u, _, f in sorted(v, key=lambda c: c[:2])] for T, v in hooks.items()}

        def unit(u):
            t, n = LAST_JOBS[u]
            return t // S, n // S, t, t % BLK, n

        block = ctx.enter_context(nc.Block())

        def raw_slot(key):
            return AT[key] % RAW

        def raw_fill(key):
            return 16 * (AT[key] // RAW + 1)

        SMALL = 5
        n_small2 = 3 * B + 1

        @block.sync
        def _(sp):
            def chunk_free(key, more=0):
                c = AT[key] - RAW
                if c < 0:
                    return
                kind, n = STREAM[c]
                if kind == "plain":
                    sp.wait_ge(w_lo, n + 1 + more)
                else:
                    sp.wait_ge(exin_lo, n + 1 + more)
                    sp.wait_ge(exout_lo, n + 1 + more)

            def load_plain(o, src):
                key = ("plain", o)
                chunk_free(key)
                sp.dma_start(raw[:, raw_slot(key)], src).then_inc(raw_full[raw_slot(key)], 16)

            def load_x(tb, o):
                key = ("plain", o)
                chunk_free(key)
                s = raw_slot(key)
                sp.dma_start(raw[:, s].rearrange("p (d n) -> p d n", d=DT),
                             xT_d[:, :, tb * BLK:(tb + 1) * BLK]).then_inc(raw_full[s], 16)

            def load_expert(tb, q, t, fixed=None):
                base = q if fixed is None else q + EX_CH * fixed
                more = 0 if fixed is not None else EX_CH * (tb - 1)
                key = ("expert", base if fixed is not None else base + EX_CH)
                chunk_free(key, more)
                s = raw_slot(key)
                sp.dma_start(raw[:, s], ex_d[t * 4 + q % 4]).then_inc(raw_full[s], 16)

            def expert_types(tb):
                t = [sp.value_load(idx[0:1, 0, bass.ds(tb * 2 + i, 1)] if not isinstance(tb, int)
                                   else idx[0:1, 0, tb * 2 + i:tb * 2 + i + 1], min_val=0, max_val=2) for i in range(2)]
                return [t[0], t[0] + 1, t[1], t[1] + 1]

            t = None
            for kind, n in STREAM[:EX_CH + PLAIN0]:
                if kind == "expert":
                    if t is None:
                        for r in range(3):
                            sp.dma_start(idx[:, r], types_row_d[r:r + 1]).then_inc(idx_full, 16)
                        sp.wait_ge(idx_full, 48)
                        t = expert_types(0)
                    load_expert(0, n, t[n // 4], fixed=0)
                elif n == 0 or n > 4 * NSH:
                    load_x(0 if n == 0 else n - 4 * NSH, n)
                else:
                    load_plain(n, sh_d[n - 1])
            with sp.Fori(1, NB - 1) as tb:
                t = expert_types(tb)
                for q in range(EX_CH):
                    load_expert(tb, q, t[q // 4])
            t = expert_types(NB - 1)
            for kind, n in STREAM[AT[("expert", 48)]:AT[("expert", 63)] + 1]:
                if kind == "expert":
                    load_expert(NB - 1, n - 48, t[(n - 48) // 4], fixed=NB - 1)
                else:
                    load_plain(n, l1_d[n - PLAIN0])
            with sp.Fori(0, 4) as i:
                for r in range(12):
                    key = ("plain", PLAIN0 + 6 + r)
                    s = raw_slot(key)
                    if r < RAW:
                        sp.wait_ge(exin_lo, 64)
                        sp.wait_ge(exout_lo, 64)
                    sp.wait_ge(w_lo, PLAIN0 + 6 + r - 3 + i * 12)
                    sp.dma_start(raw[:, s], l1_d[i * 12 + 6 + r]).then_inc(raw_full[s], 16)
            langs = [sp.value_load(idx[0:1, 1, b:b + 1], min_val=0, max_val=w1_d.shape[0] - 1) for b in range(B)]
            subjs = [sp.value_load(idx[0:1, 2, b:b + 1], min_val=0, max_val=w3_d.shape[0] - 1) for b in range(B)]
            sp.wait_ge(x_mixed, NB)
            sp.dma_start(ident[:], ident_d).then_inc(small_full, 16)
            for b in range(B):
                key = ("plain", PLAIN0 + 6 * NE1 + b)
                chunk_free(key)
                s = raw_slot(key)
                sp.dma_start(raw[:, s, 0:512], w3_d[subjs[b]]).then_inc(raw_full[s], 16)
                sp.dma_start(raw[:, s, 512:640], w1_d[langs[b]]).then_inc(raw_full[s], 16)
                sp.dma_start(raw[0:A2, s, 640:896], w2_d[langs[b]]).then_inc(raw_full[s], 16)
                sp.dma_start(cols[:, b], cols_d[langs[b]]).then_inc(small_full, 16)
                sp.dma_start(b1[:, b:b + 1], b1_d[langs[b]]).then_inc(small_full, 16)
                sp.dma_start(biasb[:, b], bias_d[subjs[b]].to_broadcast([P, D])).then_inc(small_full, 16)
            for i in range(len(LAST_JOBS)):
                _, _, t, c, n = unit(i)
                sp.wait_ge(out_ready, i + 1)
                sp.dma_start(out_d[t:t + n].rearrange("(q p) n -> p q n", p=P),
                             ostage[:, i % 2, c // P:(c + n) // P]).then_inc(stored[i % 2], 16)
            sp.wait_ge(stored[0], 48)
            sp.wait_ge(stored[1], 32)

        @block.tensor
        def _(pe):
            def product(out, wh, wl, vh, vl, start, stop):
                pe.matmul(out, wh, vh, start=start, stop=False)
                pe.matmul(out, wh, vl, start=False, stop=False)
                return pe.matmul(out, wl, vh, start=False, stop=stop)

            def x_block(tb, dt, half, n, t):
                lo = tb * BLK + half * S
                sl = slice(lo, lo + n) if isinstance(tb, int) else bass.ds(lo, n)
                return t[:, dt, sl]

            def l0_up(tb, n, first):
                job, f = L0_JOBS[n // FT], n % FT
                step = tb * L0_STEPS + n
                if n == 0 and not first:
                    pe.wait_ge(w_lo, 1 + 4 * NSH + tb)
                if first and job[0] == "shared" and f % 4 == 0:
                    if n == 0:
                        pe.wait_ge(w_lo, 1)
                    pe.wait_ge(w_lo, 1 + 4 * job[1] + 2 * (f // 4) + 1)
                if not (first and n < 4):
                    pe.wait_ge(hid_lo, step - 3)
                if job[0] == "shared":
                    N, half = BLK, 0
                    wt = lambda hl, dt: W[:, 2 * job[1], hl, f * D + dt * P:f * D + (dt + 1) * P]
                else:
                    N, half = S, job[1] // 2
                    q = (FT * job[1] + f) // 2
                    if f % 2 == 0:
                        pe.wait_ge(exin_lo, q + 1 + tb * EX_CH)
                    wt = lambda hl, dt: exin[:, q % 2, hl, f % 2 * D + dt * P:f % 2 * D + (dt + 1) * P]
                out = up_ps[:, n % 4, 0:N]
                for dt in range(DT):
                    last = product(out, wt(0, dt), wt(1, dt), x_block(tb, dt, half, N, xh), x_block(tb, dt, half, N, xl),
                                   dt == 0, dt == DT - 1)
                last.then_inc(up_done, 1)

            def l0_down(tb, n, first):
                jj, f = n // FT, n % FT
                job = L0_JOBS[jj]
                step = tb * L0_STEPS + n
                pe.wait_ge(hid_lo, step + 1)
                if f == 0:
                    before = [i for i in range(jj) if SUMS[i] == SUMS[jj]]
                    if before:
                        pe.wait_ge(sum_taken, NJ * tb + before[-1] + 1)
                    elif not first:
                        back = [i for i in range(NJ) if SUMS[i] == SUMS[jj]][-1]
                        pe.wait_ge(sum_taken, NJ * tb - NJ + back + 1)
                    if jj == 1 and not first:
                        pe.wait_ge(gate_shift, tb)
                c = slice(0, BLK) if job[0] == "shared" else ex_slot(n)
                if job[0] == "shared":
                    N = BLK
                    if first and f % 4 == 0:
                        pe.wait_ge(w_lo, 1 + 4 * job[1] + 2 * (f // 4) + 2)
                    wt = lambda hl, dt: W[:, 2 * job[1] + 1, hl, f * D + dt * P:f * D + (dt + 1) * P]
                else:
                    N = S
                    q = (FT * job[1] + f) // 2
                    if f % 2 == 0:
                        pe.wait_ge(exout_lo, q + 1 + tb * EX_CH)
                    wt = lambda hl, dt: exout[:, q % 2, hl, f % 2 * D + dt * P:f % 2 * D + (dt + 1) * P]
                for dt in range(DT):
                    last = product(sums[SUMS[jj]][:, dt, 0:N], wt(0, dt), wt(1, dt), hid[:, n % 2, 0, c], hid[:, n % 2, 1, c],
                                   f == 0, f == FT - 1)
                last.then_inc(down_done, 1)

            def gate_first(tb):
                pe.wait_ge(gate_part, tb)
                for m in range(2):
                    for b in range(2):
                        c = 2 * m + b
                        last = pe.matmul(gate_ps(tb)[:, 0, c:c + 1], gpart[:, b, m * P:(m + 1) * P], ones[:, 0:1],
                                         start=True, stop=True)
                last.then_inc(gate_up, 1)

            def gate_second(tb):
                pe.wait_ge(gate_prod, tb)
                for m in range(2):
                    last = pe.matmul(gate_ps(tb)[:, 1, 0:8], ones[:], gprod[:, m].rearrange("p b c -> p (b c)"),
                                     start=m == 0, stop=m == 1)
                last.then_inc(gate_logits, 1)

            def l0_block(tb, first=False):
                for n in range(L0_STEPS):
                    l0_up(tb, n, first)
                    if n >= 2:
                        l0_down(tb, n - 2, first)
                    elif not first:
                        l0_down(tb - 1, L0_STEPS + n - 2, first)
                    if not first and n == 3:
                        gate_first(tb)
                    if not first and n == 4:
                        gate_second(tb)

            def l1_up(e, par, n, tok, N):
                t, f = e * L1_STEPS + n, n % FT
                if isinstance(e, int) and t < 2:
                    pe.wait_ge(hid_lo, L0_ALL + t - 1)
                else:
                    pe.wait_ge(gated_done, t - 1)
                if n in (0, 4):
                    pe.wait_ge(w_lo, PLAIN0 + 6 * e + 3 * (f // 4) + 2)
                if isinstance(e, int) and e == 0 and f == 0:
                    pe.wait_ge(x_lo, n // FT + 1)
                for m in range(2):
                    ps = up_ps[:, 2 * m + f % 2, :] if N == BLK else up_ps[:, f % 2, m * S:(m + 1) * S]
                    for dt in range(DT):
                        c = slice(f * D + dt * P, f * D + (dt + 1) * P)
                        last = product(ps, W[:, 3 * par + m, 0, c], W[:, 3 * par + m, 1, c],
                                       xh[:, dt, tok:tok + N], xl[:, dt, tok:tok + N], dt == 0, dt == DT - 1)
                last.then_inc(up_done, 1)

            def l1_down(e, par, n, N):
                pe.wait_ge(hid_lo, L0_ALL + e * L1_STEPS + n + 1)
                job, f = n // FT, n % FT
                last_e = isinstance(e, int) and e == NE1 - 1
                if f == 0:
                    if isinstance(e, int) and e == 0 and job == 1:
                        pe.wait_ge(gate_shift, NB)
                    pe.wait_ge(sum_taken, NB * NJ + 4 * e + job - (0 if last_e and job else 1))
                if n in (0, 4):
                    pe.wait_ge(w_lo, PLAIN0 + 6 * e + 3 * (f // 4) + 3)
                for dt in range(DT):
                    c = slice(f * D + dt * P, f * D + (dt + 1) * P)
                    last = product(l1_sum(job, last_e)[:, dt, 0:N], W[:, 3 * par + 2, 0, c], W[:, 3 * par + 2, 1, c],
                                   hid[:, f % 2, 0, 0:N], hid[:, f % 2, 1, 0:N], f == 0, f == FT - 1)
                last.then_inc(down_done, 1)

            def l1_expert(e, par, first=False):
                for n in range(L1_STEPS):
                    l1_up(e, par, n, n // FT * BLK, BLK)
                    if n >= 2:
                        l1_down(e, par, n - 2, BLK)
                    elif not first:
                        l1_down(e - 1, 1 - par, L1_STEPS + n - 2, BLK)
                    else:
                        l0_down(NB - 1, L0_STEPS + n - 2, False)
                    if first and n == 3:
                        gate_first(NB)
                    if first and n == 4:
                        gate_second(NB)

            def l2_up_stage(i):
                b0, nb, t0, c0, n = unit(i)
                pe.wait_ge(x2_lo, i + 1)
                pe.wait_ge(w_lo, PLAIN0 + 6 * NE1 + b0 + nb)
                if i in (1, 2):
                    pe.wait_ge(out_ready, i)
                if i == 4:
                    pe.wait_ge(out_ready, 3)
                for b in range(b0, b0 + nb):
                    t, c = slice(b * S, (b + 1) * S), slice(b % 2 * S, (b % 2 + 1) * S)
                    for dt in range(DT):
                        m = slice(dt * A2, (dt + 1) * A2)
                        last = product(unit_ps[i][0:A2, 0, c], w1r[:, b, 0, m], w1r[:, b, 1, m],
                                       xh[:, dt, t], xl[:, dt, t], dt == 0, dt == DT - 1)
                last.then_inc(l2_up, 1)

            def l2_down_stage(i):
                b0, nb, t0, c0, n = unit(i)
                pe.wait_ge(l2_hid, i + 1)
                for b in range(b0, b0 + nb):
                    c = slice(b % 2 * S, (b % 2 + 1) * S)
                    for dt in range(DT):
                        m = slice(dt * P, (dt + 1) * P)
                        last = product(unit_ps[i][:, dt, c], w2[:, b, 0, m], w2[:, b, 1, m], u[:, 0, c], u[:, 1, c], True, True)
                last.then_inc(l2_down, 1)

            def mean_stage(i):
                b0, nb, t0, c0, n = unit(i)
                pe.wait_ge(y_done, i + 1)
                for dt in range(DT):
                    last = pe.matmul(unit_ps[i][:, 0, c0:c0 + n], ones[:], y[:, dt, c0:c0 + n], start=dt == 0, stop=dt == DT - 1)
                last.then_inc(mean_done, 1)

            def var_stage(i):
                b0, nb, t0, c0, n = unit(i)
                pe.wait_ge(sq_done, i + 1)
                for q in range(c0 // P, (c0 + n) // P):
                    for dt in range(DT):
                        last = pe.matmul(unit_ps[i][:, 1, q:q + 1], sq[:, dt, q * P:(q + 1) * P], ones[:, 0:1],
                                         start=dt == 0, stop=dt == DT - 1)
                last.then_inc(var_done, 1)

            def rstd_stage(i):
                b0, nb, t0, c0, n = unit(i)
                pe.wait_ge(diag_done, i + 1)
                pe.matmul(unit_ps[i][:, 1, c0:c0 + n], ones[:],
                          diag[:, c0 // P:(c0 + n) // P].rearrange("p q n -> p (q n)"),
                          start=True, stop=True).then_inc(rstd_bc, 1)

            def l3_stage(i):
                b0, nb, t0, c0, n = unit(i)
                pe.wait_ge(x3_lo, i + 1)
                for q in range(c0 // P, (c0 + n) // P):
                    b = b0 + (q - c0 // P) // 2
                    t = slice(t0 - c0 + q * P, t0 - c0 + (q + 1) * P)
                    out = unit_ps[i][:, q // 2, q % 2 * D:(q % 2 + 1) * D]
                    for dt in range(DT):
                        c = slice(dt * D, (dt + 1) * D)
                        pe.matmul(out, xh[:, dt, t], w3[:, b, 0, c], start=dt == 0, stop=False)
                        pe.matmul(out, xh[:, dt, t], w3[:, b, 1, c], start=False, stop=False)
                        pe.matmul(out[:, dt * P:(dt + 1) * P], xh[:, dt, t], identr[:], start=False, stop=False,
                                  skip_group_check=True)
                        pe.matmul(out[:, dt * P:(dt + 1) * P], xl[:, dt, t], identr[:], start=False, stop=False,
                                  skip_group_check=True)
                        last = pe.matmul(out, xl[:, dt, t], w3[:, b, 0, c], start=False, stop=dt == DT - 1)
                last.then_inc(l3_done, 1)

            l0_block(0, first=True)
            with pe.Fori(1, NB - 1) as tb:
                l0_block(tb)
            l0_block(NB - 1)
            l1_expert(0, 0, first=True)
            l1_expert(1, 1)
            with pe.Fori(1, 4) as i:
                l1_expert(i * 2, 0)
                l1_expert(i * 2 + 1, 1)
            hooks = placed({"up": l2_up_stage, "down": l2_down_stage, "mean": mean_stage, "var": var_stage,
                            "rstd": rstd_stage, "l3": l3_stage})

            def last_step(T, tok, N):
                l1_up(NE1 - 1, 0, T, tok, N)
                if T < 2:
                    l1_down(NE1 - 2, 1, L1_STEPS + T - 2, BLK)
                else:
                    l1_down(NE1 - 1, 0, T - 2, LAST_JOBS[(T - 2) // FT][1])

            last_steps(last_step, hooks)
            for T in range(40, 60):
                if T < 42:
                    l1_down(NE1 - 1, 0, T - 2, S)
                for h in hooks.get(T, []):
                    h()

        @block.scalar
        def _(act):
            A = nc.scalar.activation

            def plain_hi(o, dst, more=0, fills=0):
                key = ("plain", o)
                act.wait_ge(raw_full[raw_slot(key)], raw_fill(key) + fills)
                src = raw[:, raw_slot(key)]
                if len(dst.shape) == 3:
                    src = src.rearrange("p (d n) -> p d n", d=DT)
                A(dst, src, ACT.Copy).then_inc(w_hi, 1)

            def shared_hi(o):
                j, r = (o - 1) // 4, (o - 1) % 4
                plain_hi(o, W[:, 2 * j + r % 2, 0, r // 2 * CH:(r // 2 + 1) * CH])

            def x_hi0(o):
                tb = 0 if o == 0 else o - 4 * NSH
                plain_hi(o, xh[:, :, tb * BLK:(tb + 1) * BLK])

            def expert_hi(ring, part, s, q, tb, loop):
                qq = q if loop else q + EX_CH * tb
                key = ("expert", qq + EX_CH if loop else qq)
                fills = 16 * (EX_CH // RAW) * (tb - 1) if loop else 0
                act.wait_ge(raw_full[raw_slot(key)], raw_fill(key) + fills)
                A(ring[:, q % 2, 0], raw[:, raw_slot(key), part * 512:(part + 1) * 512], ACT.Copy).then_inc(s, 1)

            def exout_hook(q, tb, loop):
                if q > 1:
                    act.wait_ge(down_done, L0_STEPS * tb + local_step(2 * q - 3) + 1)
                elif not (isinstance(tb, int) and tb == 0):
                    act.wait_ge(down_done, L0_STEPS * tb)
                expert_hi(exout, 1, exout_hi, q, tb, loop)

            def mixed_hi(tb):
                act.wait_ge(x_mixed, tb)
                p = (tb - 1) * BLK
                sl = slice(p, p + BLK) if isinstance(tb, int) else bass.ds(p, BLK)
                A(xh[:, :, sl], x[:, :, sl], ACT.Copy).then_inc(x_hi, 1)

            def gate_exps(tb):
                act.wait_ge(gate_shift, tb)
                A(gexp[:].rearrange("p b c -> p (b c)"), gexp[:].rearrange("p b c -> p (b c)"), ACT.Exp).then_inc(gate_exp, 1)

            def l0_block(tb, hooks, first=False, last_block=False):
                loop = not isinstance(tb, int)
                for n in range(L0_STEPS):
                    kind, j = L0_JOBS[n // FT]
                    N = BLK if kind == "shared" else S
                    step = L0_STEPS * tb + n
                    act.wait_ge(up_done, step + 1)
                    if kind == "expert" and n % FT >= 2:
                        act.wait_ge(down_done, step - 3)
                    elif not (first and n < 2):
                        act.wait_ge(down_done, step - 1)
                    c = slice(0, BLK) if kind == "shared" else ex_slot(n)
                    A(hid[:, n % 2, 0, c], up_ps[:, n % 4, 0:N], ACT.Relu).then_inc(hid_hi, 1)
                    k = FT * j + n % FT
                    if kind == "expert" and k % 2 == 1:
                        m = k // 2
                        if not (last_block and m >= EX_CH - 2):
                            expert_hi(exin, 0, exin_hi, m + 2, tb, loop)
                    if kind == "expert" and exout_at(k, first, last_block) is not None:
                        exout_hook(exout_at(k, first, last_block), tb, loop)
                    if not first and n == 4:
                        gate_exps(tb)
                    if not first and n == 4 * FT:
                        mixed_hi(tb)
                    for h in hooks.get(n, []):
                        h()

            for dst, src in ((types, types_d), (gvec, gvec_d), (sg, sgate_d), (prob, prob_d), (gw2, gw2_d)):
                act.dma_start(dst[:], src).then_inc(const_full, 16)

            def vec_exp():
                act.wait_ge(softp, 1)
                A(gp[:], gp[:], ACT.Exp, scale=10.0).then_inc(softe, 1)

            act.dma_start(gw1[:], gw1_d).then_inc(gw1_full, 16)
            x_hi0(0)
            shared_hi(1)
            hooks = {n: [lambda o=n + 2: shared_hi(o)] for n in range(6)}
            hooks[6] = [lambda: expert_hi(exin, 0, exin_hi, 0, 0, False), lambda: expert_hi(exout, 1, exout_hi, 0, 0, False)]
            hooks[7] = [lambda: expert_hi(exin, 0, exin_hi, 1, 0, False)]
            for i in range(5):
                hooks[16 + i] = [lambda i=i: shared_hi(8 + i)]
            hooks[18].insert(0, lambda: exout_hook(5, 0, False))
            hooks[1].append(vec_exp)
            for i in range(3):
                hooks[21 + i] = [lambda i=i: x_hi0(13 + i)]
            l0_block(0, hooks, first=True)
            with act.Fori(1, NB - 1) as tb:
                l0_block(tb, {})

            def l1_weights_hi(e, r, par, more=0, fills=0):
                plain_hi(PLAIN0 + 6 * e + r, W[:, 3 * par + r % 3, 0, r // 3 * CH:(r // 3 + 1) * CH], more, fills)

            hooks = {FT * 4 + 2 + r: [lambda r=r: l1_weights_hi(0, r, 0)] for r in range(6)}
            hooks[FT * 4 + 2].insert(0, lambda: exout_hook(9, NB - 1, False))
            l0_block(NB - 1, hooks, last_block=True)

            def l1_step(e, n, N):
                t, f = e * L1_STEPS + n, n % FT
                act.wait_ge(up_done, L0_ALL + t + 1)
                if not (isinstance(e, int) and t < 2):
                    act.wait_ge(gated_done, t - 1)
                A(sil[:, f % 2, 0:N], up_ps[:, f % 2, 0:N], ACT.Silu).then_inc(silu_done, 1)
                act.wait_ge(gated_done, t + 1)
                act.wait_ge(down_done, L0_ALL + t - 1)
                A(hid[:, f % 2, 0, 0:N], gat[:, f % 2, 0:N], ACT.Copy).then_inc(hid_hi, 1)

            def l1_expert(e, hooks, first=False):
                for n in range(L1_STEPS):
                    l1_step(e, n, BLK)
                    if first and n == 4:
                        gate_exps(NB)
                    if first and n == 2 * FT + 6:
                        mixed_hi(NB)
                    for h in hooks.get(n, []):
                        h()

            def next_weights(e, par, base, i):
                return {4 * (r + 1): [lambda r=r: l1_weights_hi(base + 1, r, 1 - par, 0, 0 if i is None else 48 * (i - 1))]
                        for r in range(6)}

            l1_expert(0, next_weights(0, 0, 0, None), first=True)
            l1_expert(1, next_weights(1, 1, 1, None))
            with act.Fori(1, 4) as i:
                l1_expert(i * 2, next_weights(None, 0, 2, i))
                l1_expert(i * 2 + 1, next_weights(None, 1, 3, i))

            def late_hi(b):
                key = ("plain", PLAIN0 + 6 * NE1 + b)
                s = raw_slot(key)
                before = sum(1 for bb in range(b) if raw_slot(("plain", PLAIN0 + 6 * NE1 + bb)) == s)
                act.wait_ge(raw_full[s], raw_fill(key) + 32 * (before + 1))
                A(w3[:, b, 0], raw[:, s, 0:512], ACT.Copy)
                A(w1r[:, b, 0], raw[:, s, 512:640], ACT.Copy)
                A(w2[:, b, 0], raw[0:A2, s, 640:896], ACT.Copy).then_inc(w_hi, 1)

            def block_hi(ready, count, done, i):
                b0, nb, t0, c0, n = unit(i)
                act.wait_ge(ready, count + i + 1)
                A(xh[:, :, t0:t0 + n], x[:, :, t0:t0 + n], ACT.Copy).then_inc(done, 1)

            def scale_stage(i):
                b0, nb, t0, c0, n = unit(i)
                act.wait_ge(sq_done, i + 1)
                if i == 0:
                    act.wait_ge(small_full, 16 * n_small2)
                for b in range(b0, b0 + nb):
                    c = slice(b % 2 * S, (b % 2 + 1) * S)
                    for dt in range(DT):
                        last = A(y[:, dt, c], y[:, dt, c], ACT.Copy, scale=cols[:, b, 2 + dt:3 + dt])
                last.then_inc(y_scaled, 1)

            hooks = placed({"x2": lambda i: block_hi(sum_taken, NB * NJ + 32, x2_hi, i), "scale": scale_stage,
                            "x3": lambda i: block_hi(x3_done, 0, x3_hi, i)})
            for b in range(B):
                hooks.setdefault(2 + b, []).insert(0, lambda b=b: late_hi(b))
            last_steps(lambda T, tok, N: l1_step(NE1 - 1, T, N), hooks)
            for T in range(40, 60):
                for h in hooks.get(T, []):
                    h()

        @block.gpsimd
        def _(pool):
            def lo_part(dst, src, hi):
                return nc.gpsimd.tensor_tensor(dst, src, hi.bitcast(f32), ALU.subtract)

            def expert_lo(q, tb, loop):
                qq = q + EX_CH if loop else q + EX_CH * tb
                s = raw_slot(("expert", qq))
                pool.wait_ge(exin_hi, q + EX_CH * tb + 1)
                lo_part(exin[:, q % 2, 1], raw[:, s, 0:512], exin[:, q % 2, 0]).then_inc(exin_lo, 1)

            def mixed_lo(tb):
                pool.wait_ge(x_hi, tb)
                p = (tb - 1) * BLK
                sl = slice(p, p + BLK) if isinstance(tb, int) else bass.ds(p, BLK)
                lo_part(xl[:, :, sl], x[:, :, sl], xh[:, :, sl]).then_inc(x_lo, 1)

            for q in range(EX_CH + 2):
                expert_lo(q, 0, False)
            with pool.Fori(1, NB - 1) as tb:
                for q in range(2, EX_CH + 2):
                    if q == 10:
                        mixed_lo(tb)
                    expert_lo(q, tb, True)
            for q in range(2, EX_CH):
                if q == 10:
                    mixed_lo(NB - 1)
                expert_lo(q, NB - 1, False)
            mixed_lo(NB)
            pool.wait_ge(consts, 1)
            for i in range(len(LAST_JOBS)):
                b0, nb, t0, c0, n = unit(i)
                q = slice(c0 // P, (c0 + n) // P)
                pool.wait_ge(var_eps, i + 1)
                nc.gpsimd.tensor_tensor(rstd[:, q], var[:, q], mhalf[:, q], ALU.pow).then_inc(rstd_done, 1)

        @block.vector
        def _(dve):
            V = nc.vector
            n_chain = [0]

            def linked(ins):
                ins.then_inc(chain, 1)
                n_chain[0] = n_chain[0] + 1
                dve.wait_ge(chain, n_chain[0])

            def plain_lo(o, dst, hi, more=0):
                key = ("plain", o)
                dve.wait_ge(w_hi, o + 1 + more)
                src = raw[:, raw_slot(key)]
                if len(dst.shape) == 3:
                    src = src.rearrange("p (d n) -> p d n", d=DT)
                V.tensor_tensor(dst, src, hi.bitcast(f32), ALU.subtract).then_inc(w_lo, 1)

            def x_or_shared_lo(o):
                if o == 0 or o > 4 * NSH:
                    tb = 0 if o == 0 else o - 4 * NSH
                    sl = slice(tb * BLK, (tb + 1) * BLK)
                    plain_lo(o, xl[:, :, sl], xh[:, :, sl])
                else:
                    j, r = (o - 1) // 4, (o - 1) % 4
                    c = slice(r // 2 * CH, (r // 2 + 1) * CH)
                    plain_lo(o, W[:, 2 * j + r % 2, 1, c], W[:, 2 * j + r % 2, 0, c])

            def l1_lo(e, r, par, more=0):
                c = slice(r // 3 * CH, (r // 3 + 1) * CH)
                plain_lo(PLAIN0 + 6 * e + r, W[:, 3 * par + r % 3, 1, c], W[:, 3 * par + r % 3, 0, c], more)

            def constants():
                dve.wait_ge(const_full, 16 * SMALL)
                V.tensor_copy(typesf[:], types[:])
                linked(V.tensor_reduce(gmax[:], gvec[:], AX.X, ALU.max))
                V.tensor_tensor(gp[:], gvec[:], gmax[:].rearrange("p (t o) -> p t o", o=1).to_broadcast([P, 3, 4]),
                                ALU.subtract).then_inc(softp, 1)
                linked(V.tensor_scalar(omg[:], sg[:], -1.0, 1.0, ALU.mult, ALU.add))
                V.tensor_tensor(coef[:, 0:NE1 - 1, :], prob[:].rearrange("p b e -> p e b"),
                                omg[:].rearrange("p (o b) -> p o b", o=1).to_broadcast([P, NE1 - 1, B]), ALU.mult)
                V.tensor_copy(coef[:, NE1 - 1, :], sg[:]).then_inc(consts, 1)

            def expert_weights():
                dve.wait_ge(softe, 1)
                linked(V.tensor_reduce(gmax[:], gp[:], AX.X, ALU.add))
                linked(V.reciprocal(gmax[:], gmax[:]))
                linked(V.tensor_tensor(gp[:], gp[:], gmax[:].rearrange("p (t o) -> p t o", o=1).to_broadcast([P, 3, 4]),
                                       ALU.mult))
                for t in range(3):
                    dst = wab if t == 0 else wtmp
                    for s in range(2):
                        last = V.tensor_scalar(dst[:, s], typesf[:], float(t), gp[:, t, t + s:t + s + 1],
                                               ALU.is_equal, ALU.mult)
                    linked(last)
                    if t:
                        linked(V.tensor_tensor(wab[:], wab[:], wtmp[:], ALU.add))

            V.memset(ones[:], 1.0)
            V.memset(mhalf[:], -0.5)
            x_or_shared_lo(0)
            x_or_shared_lo(1)

            def l0_take(tb, jj):
                kind, j = L0_JOBS[jj]
                pair = sums[SUMS[jj]]
                dve.wait_ge(down_done, L0_STEPS * tb + FT * (jj + 1))
                if kind == "shared":
                    V.tensor_copy(acc[:, j], pair[:]).then_inc(sum_taken, 1)
                    return
                b, s = j // 2, j % 2
                if s == 1:
                    dve.wait_ge(sum_taken, NJ * tb + jj)
                p = tb * BLK + b * S
                dyn = not isinstance(tb, int)
                ex = x[:, :, bass.ds(p, S)] if dyn else x[:, :, p:p + S]
                w = wab[:, s, bass.ds(tb * 2 + b, 1)] if dyn else wab[:, s, 2 * tb + b:2 * tb + b + 1]
                if s == 0:
                    V.tensor_scalar(ex, pair[:, :, 0:S], w, None, ALU.mult).then_inc(sum_taken, 1)
                else:
                    V.scalar_tensor_tensor(ex, pair[:, :, 0:S], w, ex, ALU.mult, ALU.add).then_inc(sum_taken, 1)

            def gate_partial(tb, k):
                w, dt = k // DT, k % DT
                for b in range(2):
                    p = tb * BLK + b * S
                    if w:
                        gi = acc[:, w - 1, dt, b * S:b * S + 1]
                    elif isinstance(tb, int):
                        gi = x[:, dt, p:p + 1]
                    else:
                        gi = x[:, dt, bass.ds(p, 1)]
                    if k == 2:
                        last = V.tensor_scalar(gpart[:, b], gw1[:, k], gi, None, ALU.mult)
                    else:
                        last = V.scalar_tensor_tensor(gpart[:, b], gw1[:, k], gi, gpart[:, b], ALU.mult, ALU.add)
                if k != 1:
                    linked(last)
                else:
                    last.then_inc(gate_part, 1)

            def gate_hidden(tb):
                dve.wait_ge(gate_up, tb)
                linked(V.tensor_scalar(r1[:].rearrange("p m b -> p (m b)"), gate_ps(tb)[:, 0, 0:4], 0.0, None, ALU.max))
                for m in range(2):
                    for b in range(2):
                        last = V.tensor_scalar(gprod[:, m, b], gw2[:, m], r1[:, m, b:b + 1], None, ALU.mult)
                last.then_inc(gate_prod, 1)

            def gate_shifted(tb):
                dve.wait_ge(gate_logits, tb)
                lg = gate_ps(tb)[:, 1, 0:8].rearrange("p (b c) -> p b c", b=2)
                linked(V.tensor_reduce(glmax[:], lg, AX.X, ALU.max))
                V.tensor_tensor(gexp[:], lg, glmax[:].rearrange("p (b o) -> p b o", o=1).to_broadcast([P, 2, 4]),
                                ALU.subtract).then_inc(gate_shift, 1)

            def gate_probs(tb):
                dve.wait_ge(gate_exp, tb)
                linked(V.tensor_reduce(gsum[:], gexp[:], AX.X, ALU.add))
                linked(V.reciprocal(gsum[:], gsum[:]))
                linked(V.tensor_tensor(g[:], gexp[:], gsum[:].rearrange("p (b o) -> p b o", o=1).to_broadcast([P, 2, 4]),
                                       ALU.mult))

            def mix(tb, part, b):
                p = (tb - 1) * BLK + b * S
                sl = slice(p, p + S) if isinstance(tb, int) else bass.ds(p, S)
                xb = x[:, :, sl]
                if part == "experts":
                    ins = V.scalar_tensor_tensor(xb, xb, g[:, b, 0:1], xh[:, :, sl].bitcast(f32), ALU.mult, ALU.add)
                elif part == "lo":
                    ins = V.tensor_tensor(xb, xb, xl[:, :, sl].bitcast(f32), ALU.add)
                else:
                    ins = V.scalar_tensor_tensor(xb, acc[:, part, :, b * S:(b + 1) * S], g[:, b, part + 1:part + 2], xb,
                                                 ALU.mult, ALU.add)
                if part != NSH - 1:
                    linked(ins)
                elif b == 1:
                    ins.then_inc(x_mixed, 1)

            MIX_LATER = {16: ("lo", 0), 18: ("lo", 1), 19: (1, 0), 20: (1, 1), 21: (2, 0), 22: (2, 1)}

            def gate_hooks(tb, n):
                if n in (1, 2):
                    if n == 1:
                        dve.wait_ge(sum_taken, NJ * tb)
                    gate_partial(tb - 1, n - 1)
                if n == 3:
                    gate_hidden(tb)
                if n == 4:
                    gate_shifted(tb)
                if n == 5:
                    gate_probs(tb)
                if n in (5, 6):
                    mix(tb, "experts", n - 5)
                    mix(tb, 0, n - 5)
                if n in MIX_LATER:
                    mix(tb, *MIX_LATER[n])

            PARTIAL_AT = {33: 2, 35: 3, 37: 4, 39: 5, 43: 6, 45: 7}
            CHAIN_OWN, CHAIN_BEFORE = 6, 1 + 1 + 1 + 3 + 8

            def l0_block(tb, hooks={}, first=False, last_block=False):
                loop = not isinstance(tb, int)
                for n in range(L0_STEPS):
                    jj = n // FT
                    kind, j = L0_JOBS[jj]
                    N = BLK if kind == "shared" else S
                    if n == 1 and not first:
                        l0_take(tb - 1, NJ - 1)
                    dve.wait_ge(hid_hi, L0_STEPS * tb + n + 1)
                    c = slice(0, BLK) if kind == "shared" else ex_slot(n)
                    V.scalar_tensor_tensor(hid[:, n % 2, 1, c], up_ps[:, n % 4, 0:N], 0.0,
                                           hid[:, n % 2, 0, c].bitcast(f32), ALU.max, ALU.subtract).then_inc(hid_lo, 1)
                    if n % FT == 1 and jj:
                        l0_take(tb, jj - 1)
                    if not first:
                        gate_hooks(tb, n)
                    if n in PARTIAL_AT:
                        if n == 33:
                            dve.wait_ge(gw1_full, 16)
                        if n == 43:
                            dve.wait_ge(sum_taken, NJ * tb + 5)
                        gate_partial(tb, PARTIAL_AT[n])
                    k = FT * j + n % FT
                    if kind == "expert" and exout_at(k, first, last_block) is not None:
                        expert_lo(exout_at(k, first, last_block), tb, loop)
                    for h in hooks.get(n, []):
                        h()

            def expert_lo(q, tb, loop):
                qq = q + EX_CH if loop else q + EX_CH * tb
                s = raw_slot(("expert", qq))
                dve.wait_ge(exout_hi, q + EX_CH * tb + 1)
                V.tensor_tensor(exout[:, q % 2, 1], raw[:, s, 512:1024], exout[:, q % 2, 0].bitcast(f32),
                                ALU.subtract).then_inc(exout_lo, 1)

            hooks = {n: [lambda o=n + 2: x_or_shared_lo(o)] for n in range(6)}
            hooks[0].append(constants)
            hooks[2].append(expert_weights)
            hooks[6] = [lambda: expert_lo(0, 0, False)]
            for i in range(5):
                hooks[16 + i] = [lambda i=i: x_or_shared_lo(8 + i)]
            for i in range(3):
                hooks[21 + i] = [lambda i=i: x_or_shared_lo(13 + i)]
            hooks[18].insert(0, lambda: expert_lo(5, 0, False))
            l0_block(0, hooks, first=True)
            c0 = n_chain[0]
            with dve.Fori(1, NB - 1) as tb:
                n_chain[0] = tb * (CHAIN_OWN + CHAIN_BEFORE) + (c0 - CHAIN_OWN - CHAIN_BEFORE)
                l0_block(tb)
            n_chain[0] = c0 + 2 * (CHAIN_OWN + CHAIN_BEFORE)
            hooks = {FT * 4 + 2 + r: [lambda r=r: l1_lo(0, r, 0)] for r in range(6)}
            hooks[FT * 4 + 2].insert(0, lambda: expert_lo(9, NB - 1, False))
            l0_block(NB - 1, hooks, last_block=True)

            def l1_take(e, job, tok, N):
                last_e = isinstance(e, int) and e == NE1 - 1
                dve.wait_ge(down_done, L0_ALL + L1_STEPS * e + FT * (job + 1))
                for h in range(N // S):
                    t = slice(tok + h * S, tok + (h + 1) * S)
                    b = tok // S + h
                    w = coef[:, e, b:b + 1] if isinstance(e, int) else coef[:, bass.ds(e, 1), b]
                    last = V.scalar_tensor_tensor(x[:, :, t], l1_sum(job, last_e)[:, :, h * S:(h + 1) * S], w, x[:, :, t],
                                                  ALU.mult, ALU.add)
                last.then_inc(sum_taken, 1)

            def l1_step(e, n, N):
                t, f = e * L1_STEPS + n, n % FT
                uu = up_ps[:, 2 + f % 2, :] if N == BLK else up_ps[:, f % 2, S:2 * S]
                dve.wait_ge(silu_done, t + 1)
                V.tensor_tensor(gat[:, f % 2, 0:N], uu, sil[:, f % 2, 0:N], ALU.mult).then_inc(gated_done, 1)
                dve.wait_ge(hid_hi, L0_ALL + t + 1)
                V.tensor_tensor(hid[:, f % 2, 1, 0:N], gat[:, f % 2, 0:N], hid[:, f % 2, 0, 0:N].bitcast(f32),
                                ALU.subtract).then_inc(hid_lo, 1)

            def l1_expert(e, hooks, first=False):
                for n in range(L1_STEPS):
                    l1_step(e, n, BLK)
                    if n == 1 and first:
                        l0_take(NB - 1, NJ - 1)
                    elif n == 1:
                        l1_take(e - 1, 3, 3 * BLK, BLK)
                    elif n % FT == 1:
                        l1_take(e, n // FT - 1, (n // FT - 1) * BLK, BLK)
                    if first:
                        gate_hooks(NB, n)
                    for h in hooks.get(n, []):
                        h()

            def next_weights(par, base, i):
                return {4 * (r + 1): [lambda r=r: l1_lo(base + 1, r, 1 - par, 0 if i is None else 12 * (i - 1))]
                        for r in range(6)}

            l1_expert(0, next_weights(0, 0, None), first=True)
            l1_expert(1, next_weights(1, 1, None))
            with dve.Fori(1, 4) as i:
                l1_expert(i * 2, next_weights(0, 2, i))
                l1_expert(i * 2 + 1, next_weights(1, 3, i))

            def late_lo(b):
                o = PLAIN0 + 6 * NE1 + b
                s = raw_slot(("plain", o))
                dve.wait_ge(w_hi, o + 1)
                V.tensor_tensor(w3[:, b, 1], raw[:, s, 0:512], w3[:, b, 0].bitcast(f32), ALU.subtract)
                V.tensor_tensor(w1r[:, b, 1], raw[:, s, 512:640], w1r[:, b, 0].bitcast(f32), ALU.subtract)
                V.tensor_tensor(w2[:, b, 1], raw[0:A2, s, 640:896], w2[:, b, 0].bitcast(f32),
                                ALU.subtract).then_inc(w_lo, 1)

            def block_lo(ready, done, i):
                b0, nb, t0, c0, n = unit(i)
                dve.wait_ge(ready, i + 1)
                V.tensor_tensor(xl[:, :, t0:t0 + n], x[:, :, t0:t0 + n], xh[:, :, t0:t0 + n].bitcast(f32),
                                ALU.subtract).then_inc(done, 1)

            def hid_stage(i):
                b0, nb, t0, c0, n = unit(i)
                dve.wait_ge(l2_up, i + 1)
                if i == 0:
                    dve.wait_ge(small_full, 16 * n_small2)
                    linked(V.tensor_copy(identr[:], ident[:]))
                for b in range(b0, b0 + nb):
                    c = slice(b % 2 * S, (b % 2 + 1) * S)
                    last = V.tensor_scalar(ru[:, c], unit_ps[i][0:A2, 0, c], b1[:, b:b + 1], 0.0, ALU.add, ALU.max)
                linked(last)
                c = slice(c0, c0 + n)
                linked(V.tensor_copy(u[:, 0, c], ru[:, c]))
                V.tensor_tensor(u[:, 1, c], ru[:, c], u[:, 0, c].bitcast(f32), ALU.subtract).then_inc(l2_hid, 1)

            def res_stage(i):
                b0, nb, t0, c0, n = unit(i)
                dve.wait_ge(l2_down, i + 1)
                for b in range(b0, b0 + nb):
                    c = slice(b % 2 * S, (b % 2 + 1) * S)
                    for dt in range(DT):
                        last = V.scalar_tensor_tensor(y[:, dt, c], unit_ps[i][:, dt, c], cols[:, b, dt:dt + 1],
                                                      x[:, dt, b * S:(b + 1) * S], ALU.add, ALU.add)
                last.then_inc(y_done, 1)

            def center_stage(i):
                b0, nb, t0, c0, n = unit(i)
                c = slice(c0, c0 + n)
                dve.wait_ge(mean_done, i + 1)
                for dt in range(DT):
                    last = V.scalar_tensor_tensor(y[:, dt, c], unit_ps[i][:, 0, c], -1.0 / D, y[:, dt, c], ALU.mult, ALU.add)
                linked(last)
                V.tensor_tensor(sq[:, :, c], y[:, :, c], y[:, :, c], ALU.mult).then_inc(sq_done, 1)

            def eps_stage(i):
                b0, nb, t0, c0, n = unit(i)
                dve.wait_ge(var_done, i + 1)
                qs = slice(c0 // P, (c0 + n) // P)
                V.tensor_scalar(var[:, qs], unit_ps[i][:, 1, qs], 1.0 / D, 1e-5, ALU.mult, ALU.add).then_inc(var_eps, 1)
                dve.wait_ge(rstd_done, i + 1)
                for q in range(c0 // P, (c0 + n) // P):
                    last = V.tensor_scalar(diag[:, q], ident[:], rstd[:, q:q + 1], None, ALU.mult)
                last.then_inc(diag_done, 1)

            def norm_stage(i):
                b0, nb, t0, c0, n = unit(i)
                c = slice(c0, c0 + n)
                dve.wait_ge(y_scaled, i + 1)
                dve.wait_ge(rstd_bc, i + 1)
                for dt in range(DT):
                    last = V.tensor_tensor(y[:, dt, c], unit_ps[i][:, 1, c], y[:, dt, c], ALU.mult)
                linked(last)
                for b in range(b0, b0 + nb):
                    c = slice(b % 2 * S, (b % 2 + 1) * S)
                    for dt in range(DT):
                        xb = x[:, dt, b * S:(b + 1) * S]
                        last = V.scalar_tensor_tensor(xb, xb, cols[:, b, 4 + dt:5 + dt], y[:, dt, c], ALU.add, ALU.add)
                last.then_inc(x3_done, 1)

            def out_stage(i):
                b0, nb, t0, c0, n = unit(i)
                dve.wait_ge(l3_done, i + 1)
                if i >= 2:
                    dve.wait_ge(stored[i % 2], 16 * (i // 2))
                for b in range(b0, b0 + nb):
                    h = b % 2
                    last = V.tensor_tensor(ostage[:, i % 2, 2 * h:2 * h + 2],
                                           unit_ps[i][:, h].rearrange("p (q n) -> p q n", q=2),
                                           biasb[:, b:b + 1].to_broadcast([P, 2, D]), ALU.add)
                last.then_inc(out_ready, 1)

            hooks = placed({"x2": lambda i: block_lo(x2_hi, x2_lo, i), "hid": hid_stage, "res": res_stage,
                            "center": center_stage, "eps": eps_stage, "norm": norm_stage,
                            "x3": lambda i: block_lo(x3_hi, x3_lo, i), "out": out_stage})
            for b in range(B):
                hooks.setdefault(2 + b, []).insert(0, lambda b=b: late_lo(b))

            def last_step(T, tok, N):
                l1_step(NE1 - 1, T, N)
                if T == 1:
                    l1_take(NE1 - 2, 3, 3 * BLK, BLK)
                elif T % FT == 1:
                    l1_take(NE1 - 1, T // FT - 1, *LAST_JOBS[T // FT - 1])

            last_steps(last_step, hooks)
            l1_take(NE1 - 1, 4, *LAST_JOBS[4])
            for T in range(40, 60):
                for h in hooks.get(T, []):
                    h()


def kernel(**inputs):
    import numpy as np
    import concourse.bacc as bacc
    from concourse import mybir
    from concourse.bass_utils import run_bass_kernel_spmd

    v = {k: np.asarray(a) for k, a in inputs.items()}

    def by_rows(w):
        n = w.shape[0]
        return w.reshape(n, DT, P, FT, P).transpose(0, 2, 3, 1, 4).reshape(n, P, FT * D)

    def by_hidden(w):
        n = w.shape[0]
        return w.reshape(n, FT, P, D).transpose(0, 2, 1, 3).reshape(n, P, FT * D)

    def chunks(mats):
        s = np.stack([m.reshape(m.shape[0], P, 2, CH) for m in mats], axis=1)
        return s.transpose(0, 3, 1, 2, 4).reshape(-1, P, CH)

    shared = chunks([by_rows(v["L0_cond_share_wi"]), by_hidden(v["L0_cond_share_wo"])])
    ei = by_rows(v["L0_cond_expert_wi"]).reshape(4, P, 4, 512)
    eo = by_hidden(v["L0_cond_expert_wo"]).reshape(4, P, 4, 512)
    experts = np.concatenate([ei, eo], axis=3).transpose(0, 2, 1, 3).reshape(16, P, CH)
    cat = lambda a, b: np.concatenate([v[a], v[b][None]], axis=0)
    l1 = chunks([by_rows(cat("L1_cond_Wg", "L1_cond_Sg")), by_rows(cat("L1_cond_Wu", "L1_cond_Su")),
                 by_hidden(cat("L1_cond_Wd", "L1_cond_Sd"))])
    col = lambda a: a.reshape(-1, DT, P).transpose(0, 2, 1)
    arrays = {
        "xT": v["x"].reshape(B * S, DT, P).transpose(2, 1, 0),
        "shared": shared, "experts": experts, "l1": l1,
        "types": np.broadcast_to(v["itok_B_0_2"], (P, B)),
        "types_row": np.stack([v["itok_B_0_2"], v["itok_B_0_8"], v["itok_B_0_7"]]),
        "gvec": np.broadcast_to(v["L0_cond_gate_vecs"], (P, 3, 4)),
        "gw1": v["L0_cond_gate_w1"].reshape(8, P, D).transpose(1, 0, 2),
        "gw2": v["L0_cond_gate_w2"].reshape(2, P, 4).transpose(1, 0, 2),
        "prob": np.broadcast_to(v["fside_Bx8_0"], (P, B, 8)),
        "sgate": np.broadcast_to(v["condB_sharedgateprob"], (P, B)),
        "w1": v["L2_cond_W1"].reshape(-1, DT, P, A2).transpose(0, 2, 1, 3).reshape(-1, P, DT * A2),
        "w2": v["L2_cond_W2"],
        "b1": v["L2_cond_b1"][:, :, None],
        "cols": np.concatenate([col(v["L2_cond_b2"]), col(v["L2_cond_gamma"]), col(v["L2_cond_beta"])], axis=2),
        "w3": v["L3_cond_weight"].transpose(0, 2, 1).reshape(-1, DT, P, D).transpose(0, 2, 1, 3).reshape(-1, P, DT * D),
        "bias": v["L3_cond_bias"][:, None, :],
        "ident": np.eye(P, dtype=np.float32),
    }
    arrays = {f"in_{k}": np.ascontiguousarray(a) for k, a in arrays.items()}
    nc = bacc.Bacc("TRN2", target_bir_lowering=False, num_devices=1)
    ap = {k[3:]: nc.dram_tensor(k, a.shape, mybir.dt.from_np(a.dtype), kind="ExternalInput").ap()
          for k, a in arrays.items()}
    out = nc.dram_tensor("out", (B * S, D), mybir.dt.float32, kind="ExternalOutput").ap()
    build(nc, ap["xT"], ap["shared"], ap["experts"], ap["l1"], ap["types"], ap["types_row"], ap["gvec"], ap["gw1"],
          ap["gw2"], ap["prob"], ap["sgate"], ap["w1"], ap["w2"], ap["b1"], ap["cols"], ap["w3"],
          ap["bias"], ap["ident"], out)
    r = run_bass_kernel_spmd(nc, [arrays], core_ids=[0])
    return r.results[0]["out"].reshape(B, S, D)
```

```python
import concourse.bass as bass
from concourse import mybir
from contextlib import ExitStack


B, S, D, F = 8, 256, 256, 1024
P = 128
DT = D // P
FT = F // P
NB = 4
BLK = B * S // NB
NSH = 3
NE1 = 9
A2 = 64
CH = 1024
RAW = 4
L0_JOBS = [("shared", 0), ("expert", 0), ("shared", 1), ("expert", 1), ("shared", 2), ("expert", 2), ("expert", 3)]
NJ = len(L0_JOBS)
L0_STEPS = NJ * FT
L0_ALL = NB * L0_STEPS
EX_STEPS = 4 * FT
EX_CH = EX_STEPS // 2
SUMS = [0, 1, 0, 1, 0, 1, 0]
PLAIN0 = 4 + 4 * NSH
LAST_JOBS = [(0, BLK), (BLK, BLK), (2 * BLK, BLK), (3 * BLK, S), (3 * BLK + S, S)]
L1_STEPS = 4 * FT
STAGES = ["x2a", "x2b", "up", "hid", "down", "res", "square", "scale", "var", "eps", "diag", "rstd",
          "norm", "add", "x3a", "x3b", "l3a", "outa", "l3b", "outb"]
WHEN = [dict(zip(STAGES, at)) for at in (
    (10, 10, 11, 11, 12, 12, 12, 13, 13, 13, 13, 14, 14, 15, 15, 15, 16, 16, 17, 18),
    (18, 18, 19, 19, 20, 20, 20, 21, 21, 21, 21, 22, 22, 23, 23, 23, 24, 25, 25, 26),
    (26, 27, 28, 28, 30, 30, 30, 31, 32, 32, 32, 34, 34, 35, 36, 36, 37, 37, 38, 38),
    (34, 34, 35, 36, 37, 37, 38, 38, 40, 40, 43, 44, 45, 48, 49, 49, 50, 52, 53, 56),
    (42, 42, 43, 44, 45, 46, 47, 49, 48, 49, 51, 52, 53, 54, 55, 55, 56, 56, 57, 57))]


def job_of_expert(j):
    return [i for i, (kind, n) in enumerate(L0_JOBS) if kind == "expert" and n == j][0]


def exout_at(k, first, last_block):
    q = (k + 1) // 2
    if k == 0 or (k % 2 == 1) != (q % 4 == 0):
        return None
    if first and q == 5 or last_block and q in (9, EX_CH):
        return None
    return q


def local_step(k):
    return FT * job_of_expert(k // FT) + k % FT


def stream_table():
    sh = lambda j, m, h: ("plain", 1 + 4 * j + 2 * h + m)
    t = [("plain", 0), sh(0, 0, 0), sh(0, 1, 0), sh(0, 0, 1), sh(0, 1, 1),
         sh(1, 0, 0), sh(1, 1, 0), sh(1, 0, 1), ("expert", 0), ("expert", 1), ("expert", 2), ("expert", 3), ("expert", 4), ("expert", 5),
         sh(1, 1, 1)] + [sh(2, m, h) for h in range(2) for m in range(2)]
    t += [("plain", 13), ("plain", 14), ("plain", 15)]
    t += [("expert", q) for q in range(6, 58)]
    t += [("plain", PLAIN0 + r) for r in range(6)]
    t += [("expert", q) for q in range(58, 64)]
    t += [("plain", PLAIN0 + r) for r in range(6, 6 * NE1 + B)]
    return t


STREAM = stream_table()
AT = {k: c for c, k in enumerate(STREAM)}


def build(nc, xT_d, sh_d, ex_d, l1_d, types_d, types_row_d, gvec_d, gw1_d, gw2_d, prob_d, sgate_d, w1_d, w2_d, b1_d, cols_d, w3_d, bias_d, ident_d, out_d):
    f32, f32r, i32 = mybir.dt.float32, mybir.dt.float32r, mybir.dt.int32
    ALU, ACT, AX = mybir.AluOpType, mybir.ActivationFunctionType, mybir.AxisListType

    size = {f32: 4, f32r: 4, i32: 4}
    top = [(nc.sbuf_base + 31) // 32 * 32]

    def place(name, shape, dt, over=None, skip=0):
        n = size[dt]
        for s in shape[1:]:
            n *= s
        if over is None:
            at = top[0]
            top[0] += (n + 31) // 32 * 32
        else:
            at = where[over] + skip
        where[name] = at
        return nc.alloc_sbuf_tensor_at(name, shape, dt, offset=at)

    where = {}
    W = place("weights", [P, 6, 2, FT * D], f32r)
    raw = place("raw", [P, RAW, CH], f32)
    exin = place("expert_in", [P, 2, 2, 512], f32r)
    exout = place("expert_out", [P, 2, 2, 512], f32r)
    x = place("x", [P, DT, B * S], f32)
    xh = place("x_hi", [P, DT, B * S], f32r)
    xl = place("x_lo", [P, DT, B * S], f32r)
    acc = place("shared_sums", [P, NSH, DT, BLK], f32)
    hid = place("hidden", [P, 2, 2, BLK], f32r)
    gw1 = place("gate_w1", [P, 8, D], f32)
    gw2 = place("gate_w2", [P, 2, 4], f32)
    ones = place("ones", [P, P], f32)
    types = place("types", [P, B], i32)
    typesf = place("types_f", [P, B], f32)
    idx = place("idx", [1, 3, B], i32)
    gvec = place("gate_vecs", [P, 3, 4], f32)
    gmax = place("gate_vec_max", [P, 3], f32)
    gp = place("gate_vec_probs", [P, 3, 4], f32)
    wab = place("expert_weight", [P, 2, B], f32)
    wtmp = place("expert_weight_part", [P, 2, B], f32)
    prob = place("prob", [P, B, NE1 - 1], f32)
    sg = place("shared_gate", [P, B], f32)
    omg = place("one_minus_gate", [P, B], f32)
    coef = place("l1_coef", [P, NE1, B], f32)
    r1 = place("gate_hidden", [P, 2, 2], f32)
    gpart = place("gate_partial", [P, 2, D], f32)
    gprod = place("gate_products", [P, 2, 4], f32)
    glmax = place("gate_logit_max", [P, 2], f32)
    gexp = place("gate_exp", [P, 2, 4], f32)
    gsum = place("gate_sum", [P, 2], f32)
    g = place("gate", [P, 2, 4], f32)
    mhalf = place("minus_half", [P, 4], f32)
    assert top[0] <= nc.sbuf_usable_end, (top[0], nc.sbuf_usable_end)
    sil = place("silu", [P, 2, BLK], f32, over="expert_in")
    gat = place("gated", [P, 2, BLK], f32, over="expert_in", skip=4 * 2 * BLK)
    ostage = place("out_stage", [P, 2, 4, D], f32, over="expert_out")
    biasb = place("l3_bias", [P, B, D], f32, over="shared_sums")
    diag = place("rstd_diag", [P, 4, P], f32, over="shared_sums", skip=4 * B * D)
    ident = place("ident", [P, P], f32, over="shared_sums", skip=4 * B * D + 16 * P)
    small = 4 * B * D + 20 * P
    cols = place("l2_cols", [P, B, 6], f32, over="shared_sums", skip=small)
    b1 = place("l2_b1", [A2, B], f32, over="shared_sums", skip=small + 192)
    var = place("variance", [P, 4], f32, over="shared_sums", skip=small + 224)
    rstd = place("rstd", [P, 4], f32, over="shared_sums", skip=small + 256)
    minus_mean = place("minus_mean", [P, P], f32r, over="shared_sums", skip=small + 288)
    b2c = place("b2_centered", [P, B, DT], f32, over="shared_sums", skip=small + 800)
    b2s = place("b2_sum", [P, B], f32, over="shared_sums", skip=small + 864)
    w2s = place("w2_sum", [A2, 1], f32, over="shared_sums", skip=small + 896)
    w1r = place("l2_w1", [P, B, 2, DT * A2], f32r, over="gate_w1")
    y = place("y", [P, DT, BLK], f32, over="raw")
    sq = place("squares", [P, DT, BLK], f32, over="raw", skip=4096)
    ru = place("l2_hidden", [A2, BLK], f32, over="raw", skip=8192)
    u = place("l2_hidden_r", [A2, 2, BLK], f32r, over="raw", skip=10240)
    w3 = W[:, 3:5].rearrange("p s h n -> p (s h n)").rearrange("p (b h n) -> p b h n", b=B, h=2)
    w2 = W[0:A2, 5].rearrange("p h n -> p (h n)").rearrange("p (b h n) -> p b h n", b=B, h=2)

    ctx = ExitStack()
    with ctx:
        def bank(name, n):
            return ctx.enter_context(nc.psum_tensor(name, [P, n, 512], f32))

        def sem(name):
            return ctx.enter_context(nc.semaphore(name))

        up_ps = bank("up", 4)
        sums = [bank("sum0", 2), bank("sum1", 2)]
        unit_ps = [sums[0], sums[0], sums[0], up_ps[:, 2:4], sums[0]]

        raw_full = [sem(f"raw_full{i}") for i in range(RAW)]
        warm = sem("warm")
        const_full, gw1_full = sem("const_full"), sem("gw1_full")
        idx_full = sem("idx_full")
        consts = sem("consts")
        softp = sem("softp")
        softe = sem("softe")
        w_hi, w_lo = sem("w_hi"), sem("w_lo")
        exin_hi, exin_lo = sem("exin_hi"), sem("exin_lo")
        exout_hi, exout_lo = sem("exout_hi"), sem("exout_lo")
        up_done, down_done = sem("up_done"), sem("down_done")
        hid_hi, hid_lo = sem("hid_hi"), sem("hid_lo")
        sum_taken = sem("sum_taken")
        silu_done, gated_done = sem("silu_done"), sem("gated_done")
        gate_part, gate_up, gate_prod, gate_logits = sem("gate_part"), sem("gate_up"), sem("gate_prod"), sem("gate_logits")
        gate_shift, gate_exp = sem("gate_shift"), sem("gate_exp")
        x_mixed, x_hi, x_lo = sem("x_mixed"), sem("x_hi_done"), sem("x_lo_done")
        chain = sem("dve_chain")
        small_full = sem("small_full")
        x2_done, x2_hi, x2_lo = sem("x2_done"), sem("x2_hi"), sem("x2_lo")
        ident_full, w3_added = sem("ident_full"), sem("w3_added")
        w2_centered, b2_sum, b2_done = sem("w2_centered"), sem("b2_sum"), sem("b2_done")
        l2_up, l2_hid, l2_down = sem("l2_up"), sem("l2_hid"), sem("l2_down")
        var_done = sem("var_done")
        centered, sq_low, sq_high = sem("centered"), sem("sq_low"), sem("sq_high")
        var_eps, rstd_done, diag_done, rstd_bc = sem("var_eps"), sem("rstd_done"), sem("diag_done"), sem("rstd_bc")
        y_scaled, normed, x3_done = sem("y_scaled"), sem("normed"), sem("x3_done")
        x3_hi, x3_lo, l3_done = sem("x3_hi"), sem("x3_lo"), sem("l3_done")
        out_ready, stored = sem("out_ready"), [sem("stored0"), sem("stored1")]

        def l1_sum(job, last_e):
            return sums[1 if last_e else (job + 1) % 2]

        def gate_ps(tb):
            return sums[0 if isinstance(tb, int) and tb == NB else 1]

        def ex_slot(n):
            return slice(n // 2 % 2 * S, (n // 2 % 2 + 1) * S)

        def last_steps(step, hooks):
            for T in range(40):
                job = T // FT
                step(T, *LAST_JOBS[job])
                for h in hooks.get(T, []):
                    h()

        def placed(stages):
            hooks = {}
            for name in STAGES:
                for u in range(len(WHEN)):
                    if name in stages:
                        hooks.setdefault(WHEN[u][name], []).append((u, STAGES.index(name), stages[name]))
            return {T: [lambda f=f, u=u: f(u) for u, _, f in sorted(v, key=lambda c: c[:2])] for T, v in hooks.items()}

        def late_step(b):
            return b + 1 if b < B - 1 else FT + 2

        def unit(u):
            t, n = LAST_JOBS[u]
            return t // S, n // S, t, t % BLK, n

        block = ctx.enter_context(nc.Block())

        def raw_slot(key):
            return AT[key] % RAW

        def raw_fill(key):
            return 16 * (AT[key] // RAW + 1)

        def late_fill(b):
            key = ("plain", PLAIN0 + 6 * NE1 + b)
            before = sum(1 for bb in range(b) if raw_slot(("plain", PLAIN0 + 6 * NE1 + bb)) == raw_slot(key))
            return raw_fill(key) + 32 * (before + 1)

        SMALL = 5
        late_small = 3 * B

        @block.sync
        def _(sp):
            def chunk_free(key, more=0):
                c = AT[key] - RAW
                if c < 0:
                    return
                kind, n = STREAM[c]
                if kind == "plain":
                    sp.wait_ge(w_lo, n + 1 + more)
                else:
                    sp.wait_ge(exin_lo, n + 1 + more)
                    sp.wait_ge(exout_lo, n + 1 + more)

            def load_plain(o, src):
                key = ("plain", o)
                chunk_free(key)
                sp.dma_start(raw[:, raw_slot(key)], src).then_inc(raw_full[raw_slot(key)], 16)

            def load_x(tb, o):
                key = ("plain", o)
                chunk_free(key)
                s = raw_slot(key)
                sp.dma_start(raw[:, s].rearrange("p (d n) -> p d n", d=DT),
                             xT_d[:, :, tb * BLK:(tb + 1) * BLK]).then_inc(raw_full[s], 16)

            def load_expert(tb, q, t, fixed=None):
                base = q if fixed is None else q + EX_CH * fixed
                more = 0 if fixed is not None else EX_CH * (tb - 1)
                key = ("expert", base if fixed is not None else base + EX_CH)
                chunk_free(key, more)
                s = raw_slot(key)
                sp.dma_start(raw[:, s], ex_d[t * 4 + q % 4]).then_inc(raw_full[s], 16)

            def expert_types(tb):
                t = [sp.value_load(idx[0:1, 0, bass.ds(tb * 2 + i, 1)] if not isinstance(tb, int)
                                   else idx[0:1, 0, tb * 2 + i:tb * 2 + i + 1], min_val=0, max_val=2) for i in range(2)]
                return [t[0], t[0] + 1, t[1], t[1] + 1]

            t = None
            for kind, n in STREAM[:EX_CH + PLAIN0]:
                if kind == "expert":
                    if t is None:
                        for r in range(3):
                            sp.dma_start(idx[:, r], types_row_d[r:r + 1]).then_inc(idx_full, 16)
                        sp.wait_ge(idx_full, 48)
                        t = expert_types(0)
                    load_expert(0, n, t[n // 4], fixed=0)
                elif n == 0 or n > 4 * NSH:
                    load_x(0 if n == 0 else n - 4 * NSH, n)
                else:
                    load_plain(n, sh_d[n - 1])
            with sp.Fori(1, NB - 1) as tb:
                t = expert_types(tb)
                for q in range(EX_CH):
                    load_expert(tb, q, t[q // 4])
            t = expert_types(NB - 1)
            for kind, n in STREAM[AT[("expert", 48)]:AT[("expert", 63)] + 1]:
                if kind == "expert":
                    load_expert(NB - 1, n - 48, t[(n - 48) // 4], fixed=NB - 1)
                else:
                    load_plain(n, l1_d[n - PLAIN0])
            with sp.Fori(0, 4) as i:
                for r in range(12):
                    key = ("plain", PLAIN0 + 6 + r)
                    s = raw_slot(key)
                    if r < RAW:
                        sp.wait_ge(exin_lo, 64)
                        sp.wait_ge(exout_lo, 64)
                    sp.wait_ge(w_lo, PLAIN0 + 6 + r - 3 + i * 12)
                    sp.dma_start(raw[:, s], l1_d[i * 12 + 6 + r]).then_inc(raw_full[s], 16)
            langs = [sp.value_load(idx[0:1, 1, b:b + 1], min_val=0, max_val=w1_d.shape[0] - 1) for b in range(B)]
            subjs = [sp.value_load(idx[0:1, 2, b:b + 1], min_val=0, max_val=w3_d.shape[0] - 1) for b in range(B)]
            sp.wait_ge(x_mixed, NB)
            sp.dma_start(ident[:], ident_d).then_inc(ident_full, 16)
            for b in range(B):
                key = ("plain", PLAIN0 + 6 * NE1 + b)
                chunk_free(key)
                s = raw_slot(key)
                sp.dma_start(raw[:, s, 0:512], w3_d[subjs[b]]).then_inc(raw_full[s], 16)
                sp.dma_start(raw[:, s, 512:640], w1_d[langs[b]]).then_inc(raw_full[s], 16)
                sp.dma_start(raw[0:A2, s, 640:896], w2_d[langs[b]]).then_inc(raw_full[s], 16)
                sp.dma_start(cols[:, b], cols_d[langs[b]]).then_inc(small_full, 16)
                sp.dma_start(b1[:, b:b + 1], b1_d[langs[b]]).then_inc(small_full, 16)
                sp.dma_start(biasb[:, b], bias_d[subjs[b]].to_broadcast([P, D])).then_inc(small_full, 16)
            for i in range(len(LAST_JOBS)):
                _, _, t, c, n = unit(i)
                for part in range(2):
                    h = n // 2
                    sp.wait_ge(out_ready, 2 * i + part + 1)
                    sp.dma_start(out_d[t + part * h:t + (part + 1) * h].rearrange("(q p) n -> p q n", p=P),
                                 ostage[:, i % 2, (c + part * h) // P:(c + (part + 1) * h) // P]).then_inc(stored[i % 2], 16)
            sp.wait_ge(stored[0], 96)
            sp.wait_ge(stored[1], 64)

        @block.tensor
        def _(pe):
            def product(out, wh, wl, vh, vl, start, stop):
                pe.matmul(out, wh, vh, start=start, stop=False)
                pe.matmul(out, wh, vl, start=False, stop=False)
                return pe.matmul(out, wl, vh, start=False, stop=stop)

            def x_block(tb, dt, half, n, t):
                lo = tb * BLK + half * S
                sl = slice(lo, lo + n) if isinstance(tb, int) else bass.ds(lo, n)
                return t[:, dt, sl]

            def l0_up(tb, n, first):
                job, f = L0_JOBS[n // FT], n % FT
                step = tb * L0_STEPS + n
                if n == 0 and not first:
                    pe.wait_ge(w_lo, 1 + 4 * NSH + tb)
                if first and job[0] == "shared" and f % 4 == 0 and n:
                    pe.wait_ge(w_lo, 1 + 4 * job[1] + 2 * (f // 4) + 1)
                if not (first and n < 4):
                    pe.wait_ge(hid_lo, step - 3)
                if job[0] == "shared":
                    N, half = BLK, 0
                    wt = lambda hl, dt: W[:, 2 * job[1], hl, f * D + dt * P:f * D + (dt + 1) * P]
                else:
                    N, half = S, job[1] // 2
                    q = (FT * job[1] + f) // 2
                    if f % 2 == 0:
                        pe.wait_ge(exin_lo, q + 1 + tb * EX_CH)
                    wt = lambda hl, dt: exin[:, q % 2, hl, f % 2 * D + dt * P:f % 2 * D + (dt + 1) * P]
                out = up_ps[:, n % 4, 0:N]
                if first and n == 0:
                    for dt in range(DT):
                        pe.wait_ge(w_hi, 2)
                        pe.matmul(out, wt(0, dt), x_block(tb, dt, half, N, xh), start=dt == 0, stop=False)
                    for dt in range(DT):
                        pe.wait_ge(w_lo, 1)
                        pe.matmul(out, wt(0, dt), x_block(tb, dt, half, N, xl), start=False, stop=False)
                    for dt in range(DT):
                        pe.wait_ge(w_lo, 2)
                        last = pe.matmul(out, wt(1, dt), x_block(tb, dt, half, N, xh), start=False, stop=dt == DT - 1)
                    last.then_inc(up_done, 1)
                    return
                for dt in range(DT):
                    last = product(out, wt(0, dt), wt(1, dt), x_block(tb, dt, half, N, xh), x_block(tb, dt, half, N, xl),
                                   dt == 0, dt == DT - 1)
                last.then_inc(up_done, 1)

            def l0_down(tb, n, first):
                jj, f = n // FT, n % FT
                job = L0_JOBS[jj]
                step = tb * L0_STEPS + n
                pe.wait_ge(hid_lo, step + 1)
                if f == 0:
                    before = [i for i in range(jj) if SUMS[i] == SUMS[jj]]
                    if before:
                        pe.wait_ge(sum_taken, NJ * tb + before[-1] + 1)
                    elif not first:
                        back = [i for i in range(NJ) if SUMS[i] == SUMS[jj]][-1]
                        pe.wait_ge(sum_taken, NJ * tb - NJ + back + 1)
                    if jj == 1 and not first:
                        pe.wait_ge(gate_shift, tb)
                c = slice(0, BLK) if job[0] == "shared" else ex_slot(n)
                if job[0] == "shared":
                    N = BLK
                    if first and f % 4 == 0:
                        pe.wait_ge(w_lo, 1 + 4 * job[1] + 2 * (f // 4) + 2)
                    wt = lambda hl, dt: W[:, 2 * job[1] + 1, hl, f * D + dt * P:f * D + (dt + 1) * P]
                else:
                    N = S
                    q = (FT * job[1] + f) // 2
                    if f % 2 == 0:
                        pe.wait_ge(exout_lo, q + 1 + tb * EX_CH)
                    wt = lambda hl, dt: exout[:, q % 2, hl, f % 2 * D + dt * P:f % 2 * D + (dt + 1) * P]
                for dt in range(DT):
                    last = product(sums[SUMS[jj]][:, dt, 0:N], wt(0, dt), wt(1, dt), hid[:, n % 2, 0, c], hid[:, n % 2, 1, c],
                                   f == 0, f == FT - 1)
                last.then_inc(down_done, 1)

            def gate_first(tb):
                pe.wait_ge(gate_part, tb)
                for m in range(2):
                    for b in range(2):
                        c = 2 * m + b
                        last = pe.matmul(gate_ps(tb)[:, 0, c:c + 1], gpart[:, b, m * P:(m + 1) * P], ones[:, 0:1],
                                         start=True, stop=True)
                last.then_inc(gate_up, 1)

            def gate_second(tb):
                pe.wait_ge(gate_prod, tb)
                pe.matmul(gate_ps(tb)[:, 1, 0:8], ones[:], gprod[:].rearrange("p b c -> p (b c)"),
                          start=True, stop=True).then_inc(gate_logits, 1)

            def l0_block(tb, first=False):
                for n in range(L0_STEPS):
                    l0_up(tb, n, first)
                    if n >= 2:
                        l0_down(tb, n - 2, first)
                    elif not first:
                        l0_down(tb - 1, L0_STEPS + n - 2, first)
                    if not first and n == 3:
                        gate_first(tb)
                    if not first and n == 4:
                        gate_second(tb)

            def l1_up(e, par, n, tok, N):
                t, f = e * L1_STEPS + n, n % FT
                if isinstance(e, int) and t < 2:
                    pe.wait_ge(hid_lo, L0_ALL + t - 1)
                else:
                    pe.wait_ge(gated_done, t - 1)
                if n in (0, 4):
                    pe.wait_ge(w_lo, PLAIN0 + 6 * e + 3 * (f // 4) + 2)
                if isinstance(e, int) and e == 0 and f == 0:
                    pe.wait_ge(x_lo, n // FT + 1)
                for m in range(2):
                    ps = up_ps[:, 2 * m + f % 2, :] if N == BLK else up_ps[:, f % 2, m * S:(m + 1) * S]
                    for dt in range(DT):
                        c = slice(f * D + dt * P, f * D + (dt + 1) * P)
                        last = product(ps, W[:, 3 * par + m, 0, c], W[:, 3 * par + m, 1, c],
                                       xh[:, dt, tok:tok + N], xl[:, dt, tok:tok + N], dt == 0, dt == DT - 1)
                last.then_inc(up_done, 1)

            def l1_down(e, par, n, N):
                pe.wait_ge(hid_lo, L0_ALL + e * L1_STEPS + n + 1)
                job, f = n // FT, n % FT
                last_e = isinstance(e, int) and e == NE1 - 1
                if f == 0:
                    if isinstance(e, int) and e == 0 and job == 1:
                        pe.wait_ge(gate_shift, NB)
                    if last_e and job:
                        pe.wait_ge(x2_done, DT * job)
                    else:
                        pe.wait_ge(sum_taken, NB * NJ + 4 * e + job - 1)
                if n in (0, 4):
                    pe.wait_ge(w_lo, PLAIN0 + 6 * e + 3 * (f // 4) + 3)
                for dt in range(DT):
                    c = slice(f * D + dt * P, f * D + (dt + 1) * P)
                    last = product(l1_sum(job, last_e)[:, dt, 0:N], W[:, 3 * par + 2, 0, c], W[:, 3 * par + 2, 1, c],
                                   hid[:, f % 2, 0, 0:N], hid[:, f % 2, 1, 0:N], f == 0, f == FT - 1)
                last.then_inc(down_done, 1)

            def l1_expert(e, par, first=False):
                for n in range(L1_STEPS):
                    l1_up(e, par, n, n // FT * BLK, BLK)
                    if n >= 2:
                        l1_down(e, par, n - 2, BLK)
                    elif not first:
                        l1_down(e - 1, 1 - par, L1_STEPS + n - 2, BLK)
                    else:
                        l0_down(NB - 1, L0_STEPS + n - 2, False)
                    if first and n == 3:
                        gate_first(NB)
                    if first and n == 4:
                        gate_second(NB)

            def b2_stage():
                pe.wait_ge(small_full, 16 * late_small)
                pe.matmul(unit_ps[0][:, 1, 0:DT * B], ones[:], cols[:, :, 0:DT], start=True, stop=True).then_inc(b2_sum, 1)

            def l2_up_stage(i):
                b0, nb, t0, c0, n = unit(i)
                pe.wait_ge(w_lo, PLAIN0 + 6 * NE1 + b0 + nb)
                if i in (1, 2):
                    pe.wait_ge(out_ready, 2 * i)
                if i == 4:
                    pe.wait_ge(out_ready, 6)
                for b in range(b0, b0 + nb):
                    t, c = slice(b * S, (b + 1) * S), slice(b % 2 * S, (b % 2 + 1) * S)
                    for dt in range(DT):
                        m = slice(dt * A2, (dt + 1) * A2)
                        if b == b0:
                            pe.wait_ge(x2_lo, DT * i + dt + 1)
                        last = product(unit_ps[i][0:A2, 0, c], w1r[:, b, 0, m], w1r[:, b, 1, m],
                                       xh[:, dt, t], xl[:, dt, t], dt == 0, dt == DT - 1)
                last.then_inc(l2_up, 1)

            def l2_down_stage(i):
                b0, nb, t0, c0, n = unit(i)
                if i == 0:
                    pe.wait_ge(b2_done, 1)
                for m in (1, 0):
                    if m == 0:
                        pe.wait_ge(l2_hid, i + 1)
                    for dt in range(DT):
                        for part in (xh, xl):
                            pe.matmul(unit_ps[i][:, m, c0:c0 + n], minus_mean[:], part[:, dt, t0:t0 + n],
                                      start=dt == 0 and part is xh, stop=False, skip_group_check=True)
                for b in range(b0, b0 + nb):
                    c = slice(b % 2 * S, (b % 2 + 1) * S)
                    for m in range(DT):
                        out, k = unit_ps[i][:, m, c], slice(m * P, (m + 1) * P)
                        pe.matmul(out, w2[:, b, 0, k], u[:, 0, c], start=False, stop=False, skip_group_check=True)
                        pe.matmul(out, w2[:, b, 0, k], u[:, 1, c], start=False, stop=False, skip_group_check=True)
                        last = pe.matmul(out, w2[:, b, 1, k], u[:, 0, c], start=False, stop=True, skip_group_check=True)
                last.then_inc(l2_down, 1)

            def var_stage(i):
                b0, nb, t0, c0, n = unit(i)
                pe.wait_ge(sq_low, i + 1)
                pe.wait_ge(sq_high, i + 1)
                for q in range(c0 // P, (c0 + n) // P):
                    for dt in range(DT):
                        last = pe.matmul(unit_ps[i][:, 1, q:q + 1], sq[:, dt, q * P:(q + 1) * P], ones[:, 0:1],
                                         start=dt == 0, stop=dt == DT - 1)
                last.then_inc(var_done, 1)

            def rstd_stage(i):
                b0, nb, t0, c0, n = unit(i)
                pe.wait_ge(diag_done, i + 1)
                pe.matmul(unit_ps[i][:, 1, c0:c0 + n], ones[:],
                          diag[:, c0 // P:(c0 + n) // P].rearrange("p q n -> p (q n)"),
                          start=True, stop=True).then_inc(rstd_bc, 1)

            def l3_stage(i, part):
                b0, nb, t0, c0, n = unit(i)
                half = n // P // 2
                for q in range(c0 // P + part * half, c0 // P + (part + 1) * half):
                    b = b0 + (q - c0 // P) // 2
                    t = slice(t0 - c0 + q * P, t0 - c0 + (q + 1) * P)
                    out = unit_ps[i][:, part, q % half * D:(q % half + 1) * D]
                    for dt in range(DT):
                        c = slice(dt * D, (dt + 1) * D)
                        if q == c0 // P:
                            pe.wait_ge(x3_lo, DT * i + dt + 1)
                        pe.matmul(out, xh[:, dt, t], w3[:, b, 0, c], start=dt == 0, stop=False)
                        pe.matmul(out, xh[:, dt, t], w3[:, b, 1, c], start=False, stop=False)
                        last = pe.matmul(out, xl[:, dt, t], w3[:, b, 0, c], start=False, stop=dt == DT - 1)
                last.then_inc(l3_done, 1)

            l0_block(0, first=True)
            with pe.Fori(1, NB - 1) as tb:
                l0_block(tb)
            l0_block(NB - 1)
            l1_expert(0, 0, first=True)
            l1_expert(1, 1)
            with pe.Fori(1, 4) as i:
                l1_expert(i * 2, 0)
                l1_expert(i * 2 + 1, 1)
            hooks = placed({"up": l2_up_stage, "down": l2_down_stage, "var": var_stage,
                            "rstd": rstd_stage, "l3a": lambda i: l3_stage(i, 0), "l3b": lambda i: l3_stage(i, 1)})
            hooks.setdefault(10, []).insert(0, b2_stage)

            def last_step(T, tok, N):
                l1_up(NE1 - 1, 0, T, tok, N)
                if T < 2:
                    l1_down(NE1 - 2, 1, L1_STEPS + T - 2, BLK)
                else:
                    l1_down(NE1 - 1, 0, T - 2, LAST_JOBS[(T - 2) // FT][1])

            last_steps(last_step, hooks)
            for T in range(40, 60):
                if T < 42:
                    l1_down(NE1 - 1, 0, T - 2, S)
                for h in hooks.get(T, []):
                    h()

        @block.scalar
        def _(act):
            A = nc.scalar.activation

            def plain_hi(o, dst, more=0, fills=0):
                key = ("plain", o)
                act.wait_ge(raw_full[raw_slot(key)], raw_fill(key) + fills)
                src = raw[:, raw_slot(key)]
                if len(dst.shape) == 3:
                    src = src.rearrange("p (d n) -> p d n", d=DT)
                A(dst, src, ACT.Copy).then_inc(w_hi, 1)

            def shared_hi(o):
                j, r = (o - 1) // 4, (o - 1) % 4
                plain_hi(o, W[:, 2 * j + r % 2, 0, r // 2 * CH:(r // 2 + 1) * CH])

            def x_hi0(o):
                tb = 0 if o == 0 else o - 4 * NSH
                plain_hi(o, xh[:, :, tb * BLK:(tb + 1) * BLK])

            def expert_hi(ring, part, s, q, tb, loop):
                qq = q if loop else q + EX_CH * tb
                key = ("expert", qq + EX_CH if loop else qq)
                fills = 16 * (EX_CH // RAW) * (tb - 1) if loop else 0
                act.wait_ge(raw_full[raw_slot(key)], raw_fill(key) + fills)
                A(ring[:, q % 2, 0], raw[:, raw_slot(key), part * 512:(part + 1) * 512], ACT.Copy).then_inc(s, 1)

            def exout_hook(q, tb, loop):
                if q > 1:
                    act.wait_ge(down_done, L0_STEPS * tb + local_step(2 * q - 3) + 1)
                elif not (isinstance(tb, int) and tb == 0):
                    act.wait_ge(down_done, L0_STEPS * tb)
                expert_hi(exout, 1, exout_hi, q, tb, loop)

            def mixed_hi(tb):
                act.wait_ge(x_mixed, tb)
                p = (tb - 1) * BLK
                sl = slice(p, p + BLK) if isinstance(tb, int) else bass.ds(p, BLK)
                A(xh[:, :, sl], x[:, :, sl], ACT.Copy).then_inc(x_hi, 1)

            def gate_exps(tb):
                act.wait_ge(gate_shift, tb)
                A(gexp[:].rearrange("p b c -> p (b c)"), gexp[:].rearrange("p b c -> p (b c)"), ACT.Exp).then_inc(gate_exp, 1)

            def l0_block(tb, hooks, first=False, last_block=False):
                loop = not isinstance(tb, int)
                for n in range(L0_STEPS):
                    kind, j = L0_JOBS[n // FT]
                    N = BLK if kind == "shared" else S
                    step = L0_STEPS * tb + n
                    act.wait_ge(up_done, step + 1)
                    if kind == "expert" and n % FT >= 2:
                        act.wait_ge(down_done, step - 3)
                    elif not (first and n < 2):
                        act.wait_ge(down_done, step - 1)
                    c = slice(0, BLK) if kind == "shared" else ex_slot(n)
                    A(hid[:, n % 2, 0, c], up_ps[:, n % 4, 0:N], ACT.Relu).then_inc(hid_hi, 1)
                    k = FT * j + n % FT
                    if kind == "expert" and k % 2 == 1:
                        m = k // 2
                        if not (last_block and m >= EX_CH - 2):
                            expert_hi(exin, 0, exin_hi, m + 2, tb, loop)
                    if kind == "expert" and exout_at(k, first, last_block) is not None:
                        exout_hook(exout_at(k, first, last_block), tb, loop)
                    if not first and n == 4:
                        gate_exps(tb)
                    if not first and n == 4 * FT:
                        mixed_hi(tb)
                    for h in hooks.get(n, []):
                        h()

            act.wait_ge(warm, 1)
            A(mhalf[:], mhalf[:], ACT.Copy).then_inc(warm, 1)

            def vec_exp():
                act.wait_ge(softp, 1)
                A(gp[:], gp[:], ACT.Exp, scale=10.0).then_inc(softe, 1)

            x_hi0(0)
            shared_hi(1)
            hooks = {n: [lambda o=n + 2: shared_hi(o)] for n in range(6)}
            hooks[6] = [lambda: expert_hi(exin, 0, exin_hi, 0, 0, False), lambda: expert_hi(exout, 1, exout_hi, 0, 0, False)]
            hooks[7] = [lambda: expert_hi(exin, 0, exin_hi, 1, 0, False)]
            for i in range(5):
                hooks[16 + i] = [lambda i=i: shared_hi(8 + i)]
            hooks[18].insert(0, lambda: exout_hook(5, 0, False))
            hooks[1].append(vec_exp)
            for i in range(3):
                hooks[21 + i] = [lambda i=i: x_hi0(13 + i)]
            l0_block(0, hooks, first=True)
            with act.Fori(1, NB - 1) as tb:
                l0_block(tb, {})

            def l1_weights_hi(e, r, par, more=0, fills=0):
                plain_hi(PLAIN0 + 6 * e + r, W[:, 3 * par + r % 3, 0, r // 3 * CH:(r // 3 + 1) * CH], more, fills)

            hooks = {FT * 4 + 2 + r: [lambda r=r: l1_weights_hi(0, r, 0)] for r in range(6)}
            hooks[FT * 4 + 2].insert(0, lambda: exout_hook(9, NB - 1, False))
            l0_block(NB - 1, hooks, last_block=True)

            def l1_step(e, n, N):
                t, f = e * L1_STEPS + n, n % FT
                act.wait_ge(up_done, L0_ALL + t + 1)
                if not (isinstance(e, int) and t < 2):
                    act.wait_ge(gated_done, t - 1)
                A(sil[:, f % 2, 0:N], up_ps[:, f % 2, 0:N], ACT.Silu).then_inc(silu_done, 1)
                act.wait_ge(gated_done, t + 1)
                act.wait_ge(down_done, L0_ALL + t - 1)
                A(hid[:, f % 2, 0, 0:N], gat[:, f % 2, 0:N], ACT.Copy).then_inc(hid_hi, 1)

            def l1_expert(e, hooks, first=False):
                for n in range(L1_STEPS):
                    l1_step(e, n, BLK)
                    if first and n == 4:
                        gate_exps(NB)
                    if first and n == 2 * FT + 3:
                        mixed_hi(NB)
                    for h in hooks.get(n, []):
                        h()

            def next_weights(e, par, base, i):
                return {4 * (r + 1): [lambda r=r: l1_weights_hi(base + 1, r, 1 - par, 0, 0 if i is None else 48 * (i - 1))]
                        for r in range(6)}

            l1_expert(0, next_weights(0, 0, 0, None), first=True)
            l1_expert(1, next_weights(1, 1, 1, None))
            with act.Fori(1, 4) as i:
                l1_expert(i * 2, next_weights(None, 0, 2, i))
                l1_expert(i * 2 + 1, next_weights(None, 1, 3, i))

            def late_hi(b):
                s = raw_slot(("plain", PLAIN0 + 6 * NE1 + b))
                act.wait_ge(raw_full[s], late_fill(b))
                act.wait_ge(w3_added, b + 1)
                A(w3[:, b, 0], raw[:, s, 0:512], ACT.Copy)
                A(w1r[:, b, 0], raw[:, s, 512:640], ACT.Copy)
                act.wait_ge(w2_centered, b + 1)
                A(w2[:, b, 0], raw[0:A2, s, 640:896], ACT.Copy).then_inc(w_hi, 1)

            def unit_hi(ready, done, i, dt):
                b0, nb, t0, c0, n = unit(i)
                act.wait_ge(ready, DT * i + dt + 1)
                A(xh[:, dt, t0:t0 + n], x[:, dt, t0:t0 + n], ACT.Copy).then_inc(done, 1)

            def scale_stage(i):
                b0, nb, t0, c0, n = unit(i)
                act.wait_ge(sq_low, i + 1)
                act.wait_ge(sq_high, i + 1)
                for b in range(b0, b0 + nb):
                    c = slice(b % 2 * S, (b % 2 + 1) * S)
                    for dt in range(DT):
                        last = A(y[:, dt, c], y[:, dt, c], ACT.Copy, scale=cols[:, b, 2 + dt:3 + dt])
                last.then_inc(y_scaled, 1)

            hooks = placed({"x2a": lambda i: unit_hi(x2_done, x2_hi, i, 0), "x2b": lambda i: unit_hi(x2_done, x2_hi, i, 1),
                            "scale": scale_stage,
                            "x3a": lambda i: unit_hi(x3_done, x3_hi, i, 0), "x3b": lambda i: unit_hi(x3_done, x3_hi, i, 1)})
            for b in range(B):
                hooks.setdefault(late_step(b), []).insert(0, lambda b=b: late_hi(b))
            last_steps(lambda T, tok, N: l1_step(NE1 - 1, T, N), hooks)
            for T in range(40, 60):
                for h in hooks.get(T, []):
                    h()

        @block.gpsimd
        def _(pool):
            def lo_part(dst, src, hi):
                return nc.gpsimd.tensor_tensor(dst, src, hi.bitcast(f32), ALU.subtract)

            def expert_lo(q, tb, loop):
                qq = q + EX_CH if loop else q + EX_CH * tb
                s = raw_slot(("expert", qq))
                pool.wait_ge(exin_hi, q + EX_CH * tb + 1)
                lo_part(exin[:, q % 2, 1], raw[:, s, 0:512], exin[:, q % 2, 0]).then_inc(exin_lo, 1)

            def mixed_lo(tb):
                pool.wait_ge(x_hi, tb)
                p = (tb - 1) * BLK
                sl = slice(p, p + BLK) if isinstance(tb, int) else bass.ds(p, BLK)
                lo_part(xl[:, :, sl], x[:, :, sl], xh[:, :, sl]).then_inc(x_lo, 1)

            for dst, src in ((types, types_d), (gvec, gvec_d), (sg, sgate_d), (prob, prob_d), (gw2, gw2_d)):
                pool.dma_start(dst[:], src).then_inc(const_full, 16)
            pool.wait_ge(w_lo, 2)
            pool.dma_start(gw1[:], gw1_d).then_inc(gw1_full, 16)
            for q in range(EX_CH + 2):
                expert_lo(q, 0, False)
            with pool.Fori(1, NB - 1) as tb:
                for q in range(2, EX_CH + 2):
                    if q == 10:
                        mixed_lo(tb)
                    expert_lo(q, tb, True)
            for q in range(2, EX_CH):
                if q == 10:
                    mixed_lo(NB - 1)
                expert_lo(q, NB - 1, False)
            mixed_lo(NB)
            pool.wait_ge(ident_full, 16)
            for b in range(B):
                s = raw_slot(("plain", PLAIN0 + 6 * NE1 + b))
                pool.wait_ge(raw_full[s], late_fill(b))
                for dt in range(DT):
                    w = raw[:, s, dt * (D + P):dt * (D + P) + P]
                    last = nc.gpsimd.tensor_tensor(w, w, ident[:], ALU.add)
                last.then_inc(w3_added, 1)
            pool.wait_ge(consts, 1)
            for i in range(len(LAST_JOBS)):
                b0, nb, t0, c0, n = unit(i)
                q = slice(c0 // P, (c0 + n) // P)
                c = slice(c0, c0 + n)
                pool.wait_ge(centered, DT * i + 1)
                nc.gpsimd.tensor_tensor(sq[:, 0, c], y[:, 0, c], y[:, 0, c], ALU.mult).then_inc(sq_low, 1)
                pool.wait_ge(var_eps, i + 1)
                nc.gpsimd.tensor_tensor(rstd[:, q], var[:, q], mhalf[:, q], ALU.pow).then_inc(rstd_done, 1)

        @block.vector
        def _(dve):
            V = nc.vector
            n_chain = [0]

            def linked(ins):
                ins.then_inc(chain, 1)
                n_chain[0] = n_chain[0] + 1
                dve.wait_ge(chain, n_chain[0])

            def plain_lo(o, dst, hi, more=0):
                key = ("plain", o)
                dve.wait_ge(w_hi, o + 1 + more)
                src = raw[:, raw_slot(key)]
                if len(dst.shape) == 3:
                    src = src.rearrange("p (d n) -> p d n", d=DT)
                V.tensor_tensor(dst, src, hi.bitcast(f32), ALU.subtract).then_inc(w_lo, 1)

            def x_or_shared_lo(o):
                if o == 0 or o > 4 * NSH:
                    tb = 0 if o == 0 else o - 4 * NSH
                    sl = slice(tb * BLK, (tb + 1) * BLK)
                    plain_lo(o, xl[:, :, sl], xh[:, :, sl])
                else:
                    j, r = (o - 1) // 4, (o - 1) % 4
                    c = slice(r // 2 * CH, (r // 2 + 1) * CH)
                    plain_lo(o, W[:, 2 * j + r % 2, 1, c], W[:, 2 * j + r % 2, 0, c])

            def l1_lo(e, r, par, more=0):
                c = slice(r // 3 * CH, (r // 3 + 1) * CH)
                plain_lo(PLAIN0 + 6 * e + r, W[:, 3 * par + r % 3, 1, c], W[:, 3 * par + r % 3, 0, c], more)

            def constants():
                dve.wait_ge(const_full, 16 * SMALL)
                V.tensor_copy(typesf[:], types[:])
                linked(V.tensor_reduce(gmax[:], gvec[:], AX.X, ALU.max))
                V.tensor_tensor(gp[:], gvec[:], gmax[:].rearrange("p (t o) -> p t o", o=1).to_broadcast([P, 3, 4]),
                                ALU.subtract).then_inc(softp, 1)
                linked(V.tensor_scalar(omg[:], sg[:], -1.0, 1.0, ALU.mult, ALU.add))
                V.tensor_tensor(coef[:, 0:NE1 - 1, :], prob[:].rearrange("p b e -> p e b"),
                                omg[:].rearrange("p (o b) -> p o b", o=1).to_broadcast([P, NE1 - 1, B]), ALU.mult)
                V.tensor_copy(coef[:, NE1 - 1, :], sg[:]).then_inc(consts, 1)

            def expert_weights():
                dve.wait_ge(softe, 1)
                linked(V.tensor_reduce(gmax[:], gp[:], AX.X, ALU.add))
                linked(V.reciprocal(gmax[:], gmax[:]))
                linked(V.tensor_tensor(gp[:], gp[:], gmax[:].rearrange("p (t o) -> p t o", o=1).to_broadcast([P, 3, 4]),
                                       ALU.mult))
                for t in range(3):
                    dst = wab if t == 0 else wtmp
                    for s in range(2):
                        last = V.tensor_scalar(dst[:, s], typesf[:], float(t), gp[:, t, t + s:t + s + 1],
                                               ALU.is_equal, ALU.mult)
                    linked(last)
                    if t:
                        linked(V.tensor_tensor(wab[:], wab[:], wtmp[:], ALU.add))

            V.memset(ones[:], 1.0)
            V.memset(mhalf[:], -0.5).then_inc(warm, 1)
            x_or_shared_lo(0)
            x_or_shared_lo(1)

            def l0_take(tb, jj):
                kind, j = L0_JOBS[jj]
                pair = sums[SUMS[jj]]
                dve.wait_ge(down_done, L0_STEPS * tb + FT * (jj + 1))
                if kind == "shared":
                    V.tensor_copy(acc[:, j], pair[:]).then_inc(sum_taken, 1)
                    return
                b, s = j // 2, j % 2
                if s == 1:
                    dve.wait_ge(sum_taken, NJ * tb + jj)
                p = tb * BLK + b * S
                dyn = not isinstance(tb, int)
                ex = x[:, :, bass.ds(p, S)] if dyn else x[:, :, p:p + S]
                w = wab[:, s, bass.ds(tb * 2 + b, 1)] if dyn else wab[:, s, 2 * tb + b:2 * tb + b + 1]
                if s == 0:
                    V.tensor_scalar(ex, pair[:, :, 0:S], w, None, ALU.mult).then_inc(sum_taken, 1)
                else:
                    V.scalar_tensor_tensor(ex, pair[:, :, 0:S], w, ex, ALU.mult, ALU.add).then_inc(sum_taken, 1)

            def gate_partial(tb, k):
                w, dt = k // DT, k % DT
                for b in range(2):
                    p = tb * BLK + b * S
                    if w:
                        gi = acc[:, w - 1, dt, b * S:b * S + 1]
                    elif isinstance(tb, int):
                        gi = x[:, dt, p:p + 1]
                    else:
                        gi = x[:, dt, bass.ds(p, 1)]
                    if k == 2:
                        last = V.tensor_scalar(gpart[:, b], gw1[:, k], gi, None, ALU.mult)
                    else:
                        last = V.scalar_tensor_tensor(gpart[:, b], gw1[:, k], gi, gpart[:, b], ALU.mult, ALU.add)
                if k != 1:
                    linked(last)
                else:
                    last.then_inc(gate_part, 1)

            def gate_hidden(tb):
                dve.wait_ge(gate_up, tb)
                linked(V.tensor_scalar(r1[:].rearrange("p m b -> p (m b)"), gate_ps(tb)[:, 0, 0:4], 0.0, None, ALU.max))
                for b in range(2):
                    last = V.tensor_scalar(gprod[:, b], gw2[:, 0], r1[:, 0, b:b + 1], None, ALU.mult)
                linked(last)
                for b in range(2):
                    last = V.scalar_tensor_tensor(gprod[:, b], gw2[:, 1], r1[:, 1, b:b + 1], gprod[:, b], ALU.mult, ALU.add)
                last.then_inc(gate_prod, 1)

            def gate_shifted(tb):
                dve.wait_ge(gate_logits, tb)
                lg = gate_ps(tb)[:, 1, 0:8].rearrange("p (b c) -> p b c", b=2)
                linked(V.tensor_reduce(glmax[:], lg, AX.X, ALU.max))
                V.tensor_tensor(gexp[:], lg, glmax[:].rearrange("p (b o) -> p b o", o=1).to_broadcast([P, 2, 4]),
                                ALU.subtract).then_inc(gate_shift, 1)

            def gate_probs(tb):
                dve.wait_ge(gate_exp, tb)
                linked(V.tensor_reduce(gsum[:], gexp[:], AX.X, ALU.add))
                linked(V.reciprocal(gsum[:], gsum[:]))
                linked(V.tensor_tensor(g[:], gexp[:], gsum[:].rearrange("p (b o) -> p b o", o=1).to_broadcast([P, 2, 4]),
                                       ALU.mult))

            def mix(tb, part, b):
                p = (tb - 1) * BLK + b * S
                sl = slice(p, p + S) if isinstance(tb, int) else bass.ds(p, S)
                xb = x[:, :, sl]
                if part == "experts":
                    ins = V.scalar_tensor_tensor(xb, xb, g[:, b, 0:1], xh[:, :, sl].bitcast(f32), ALU.mult, ALU.add)
                elif part == "lo":
                    ins = V.tensor_tensor(xb, xb, xl[:, :, sl].bitcast(f32), ALU.add)
                else:
                    ins = V.scalar_tensor_tensor(xb, acc[:, part, :, b * S:(b + 1) * S], g[:, b, part + 1:part + 2], xb,
                                                 ALU.mult, ALU.add)
                if part != NSH - 1:
                    linked(ins)
                elif b == 1:
                    ins.then_inc(x_mixed, 1)

            MIX_LATER = {16: ("lo", 0), 18: ("lo", 1), 19: (1, 0), 20: (1, 1), 21: (2, 0), 22: (2, 1)}

            def gate_hooks(tb, n):
                if n in (1, 2):
                    if n == 1:
                        dve.wait_ge(sum_taken, NJ * tb)
                    gate_partial(tb - 1, n - 1)
                if n == 3:
                    gate_hidden(tb)
                if n == 4:
                    gate_shifted(tb)
                if n == 5:
                    gate_probs(tb)
                if n in (5, 6):
                    mix(tb, "experts", n - 5)
                    mix(tb, 0, n - 5)
                later = n + 4 if isinstance(tb, int) and tb == NB else n
                if later in MIX_LATER:
                    mix(tb, *MIX_LATER[later])

            PARTIAL_AT = {33: 2, 35: 3, 37: 4, 39: 5, 43: 6, 45: 7}
            CHAIN_OWN, CHAIN_BEFORE = 6, 1 + 2 + 1 + 3 + 8

            def l0_block(tb, hooks={}, first=False, last_block=False):
                loop = not isinstance(tb, int)
                for n in range(L0_STEPS):
                    jj = n // FT
                    kind, j = L0_JOBS[jj]
                    N = BLK if kind == "shared" else S
                    if n == 1 and not first:
                        l0_take(tb - 1, NJ - 1)
                    dve.wait_ge(hid_hi, L0_STEPS * tb + n + 1)
                    c = slice(0, BLK) if kind == "shared" else ex_slot(n)
                    V.scalar_tensor_tensor(hid[:, n % 2, 1, c], up_ps[:, n % 4, 0:N], 0.0,
                                           hid[:, n % 2, 0, c].bitcast(f32), ALU.max, ALU.subtract).then_inc(hid_lo, 1)
                    if n % FT == 1 and jj:
                        l0_take(tb, jj - 1)
                    if not first:
                        gate_hooks(tb, n)
                    if n in PARTIAL_AT:
                        if n == 33:
                            dve.wait_ge(gw1_full, 16)
                        if n == 43:
                            dve.wait_ge(sum_taken, NJ * tb + 5)
                        gate_partial(tb, PARTIAL_AT[n])
                    k = FT * j + n % FT
                    if kind == "expert" and exout_at(k, first, last_block) is not None:
                        expert_lo(exout_at(k, first, last_block), tb, loop)
                    for h in hooks.get(n, []):
                        h()

            def expert_lo(q, tb, loop):
                qq = q + EX_CH if loop else q + EX_CH * tb
                s = raw_slot(("expert", qq))
                dve.wait_ge(exout_hi, q + EX_CH * tb + 1)
                V.tensor_tensor(exout[:, q % 2, 1], raw[:, s, 512:1024], exout[:, q % 2, 0].bitcast(f32),
                                ALU.subtract).then_inc(exout_lo, 1)

            hooks = {n: [lambda o=n + 2: x_or_shared_lo(o)] for n in range(6)}
            hooks[0].append(constants)
            hooks[2].append(expert_weights)
            hooks[6] = [lambda: expert_lo(0, 0, False)]
            for i in range(5):
                hooks[16 + i] = [lambda i=i: x_or_shared_lo(8 + i)]
            for i in range(3):
                hooks[21 + i] = [lambda i=i: x_or_shared_lo(13 + i)]
            hooks[18].insert(0, lambda: expert_lo(5, 0, False))
            l0_block(0, hooks, first=True)
            c0 = n_chain[0]
            with dve.Fori(1, NB - 1) as tb:
                n_chain[0] = tb * (CHAIN_OWN + CHAIN_BEFORE) + (c0 - CHAIN_OWN - CHAIN_BEFORE)
                l0_block(tb)
            n_chain[0] = c0 + 2 * (CHAIN_OWN + CHAIN_BEFORE)
            hooks = {FT * 4 + 2 + r: [lambda r=r: l1_lo(0, r, 0)] for r in range(6)}
            hooks[FT * 4 + 2].insert(0, lambda: expert_lo(9, NB - 1, False))
            l0_block(NB - 1, hooks, last_block=True)

            def l1_take(e, job, tok, N):
                last_e = isinstance(e, int) and e == NE1 - 1
                dve.wait_ge(down_done, L0_ALL + L1_STEPS * e + FT * (job + 1))
                if last_e:
                    for dt in range(DT):
                        for h in range(N // S):
                            xb = x[:, dt, tok + h * S:tok + (h + 1) * S]
                            b = tok // S + h
                            last = V.scalar_tensor_tensor(xb, l1_sum(job, True)[:, dt, h * S:(h + 1) * S],
                                                          coef[:, e, b:b + 1], xb, ALU.mult, ALU.add)
                        last.then_inc(x2_done, 1)
                    return
                for h in range(N // S):
                    t = slice(tok + h * S, tok + (h + 1) * S)
                    b = tok // S + h
                    w = coef[:, e, b:b + 1] if isinstance(e, int) else coef[:, bass.ds(e, 1), b]
                    last = V.scalar_tensor_tensor(x[:, :, t], l1_sum(job, last_e)[:, :, h * S:(h + 1) * S], w, x[:, :, t],
                                                  ALU.mult, ALU.add)
                last.then_inc(sum_taken, 1)

            def l1_step(e, n, N, take=None):
                t, f = e * L1_STEPS + n, n % FT
                uu = up_ps[:, 2 + f % 2, :] if N == BLK else up_ps[:, f % 2, S:2 * S]
                dve.wait_ge(silu_done, t + 1)
                V.tensor_tensor(gat[:, f % 2, 0:N], uu, sil[:, f % 2, 0:N], ALU.mult).then_inc(gated_done, 1)
                if take is not None:
                    l1_take(*take)
                dve.wait_ge(hid_hi, L0_ALL + t + 1)
                V.tensor_tensor(hid[:, f % 2, 1, 0:N], gat[:, f % 2, 0:N], hid[:, f % 2, 0, 0:N].bitcast(f32),
                                ALU.subtract).then_inc(hid_lo, 1)

            def l1_expert(e, hooks, first=False):
                for n in range(L1_STEPS):
                    l1_step(e, n, BLK)
                    if n == 1 and first:
                        l0_take(NB - 1, NJ - 1)
                    elif n == 1:
                        l1_take(e - 1, 3, 3 * BLK, BLK)
                    elif n % FT == 1:
                        l1_take(e, n // FT - 1, (n // FT - 1) * BLK, BLK)
                    if first:
                        gate_hooks(NB, n)
                    for h in hooks.get(n, []):
                        h()

            def next_weights(par, base, i):
                return {4 * (r + 1): [lambda r=r: l1_lo(base + 1, r, 1 - par, 0 if i is None else 12 * (i - 1))]
                        for r in range(6)}

            l1_expert(0, next_weights(0, 0, None), first=True)
            l1_expert(1, next_weights(1, 1, None))
            with dve.Fori(1, 4) as i:
                l1_expert(i * 2, next_weights(0, 2, i))
                l1_expert(i * 2 + 1, next_weights(1, 3, i))

            def center_w2(b):
                s = raw_slot(("plain", PLAIN0 + 6 * NE1 + b))
                dve.wait_ge(raw_full[s], late_fill(b))
                w = raw[0:A2, s, 640:896]
                linked(V.tensor_reduce(w2s[:], w, AX.X, ALU.add))
                V.scalar_tensor_tensor(w, w2s[:].to_broadcast([A2, D]), -1.0 / D, w, ALU.mult,
                                       ALU.add).then_inc(w2_centered, 1)

            def center_b2():
                V.tensor_scalar(minus_mean[:], ones[:], -1.0 / D, None, ALU.mult)
                dve.wait_ge(b2_sum, 1)
                linked(V.tensor_reduce(b2s[:], unit_ps[0][:, 1, 0:DT * B].rearrange("p (b t) -> p b t", t=DT), AX.X, ALU.add))
                V.scalar_tensor_tensor(b2c[:], b2s[:].rearrange("p (b t) -> p b t", t=1).to_broadcast([P, B, DT]),
                                       -1.0 / D, cols[:, :, 0:DT], ALU.mult, ALU.add).then_inc(b2_done, 1)

            def late_lo(b):
                o = PLAIN0 + 6 * NE1 + b
                s = raw_slot(("plain", o))
                dve.wait_ge(w_hi, o + 1)
                V.tensor_tensor(w3[:, b, 1], raw[:, s, 0:512], w3[:, b, 0].bitcast(f32), ALU.subtract)
                V.tensor_tensor(w1r[:, b, 1], raw[:, s, 512:640], w1r[:, b, 0].bitcast(f32), ALU.subtract)
                V.tensor_tensor(w2[:, b, 1], raw[0:A2, s, 640:896], w2[:, b, 0].bitcast(f32),
                                ALU.subtract).then_inc(w_lo, 1)

            def unit_lo(ready, done, i, dt):
                b0, nb, t0, c0, n = unit(i)
                dve.wait_ge(ready, DT * i + dt + 1)
                V.tensor_tensor(xl[:, dt, t0:t0 + n], x[:, dt, t0:t0 + n], xh[:, dt, t0:t0 + n].bitcast(f32),
                                ALU.subtract).then_inc(done, 1)

            def hid_stage(i):
                b0, nb, t0, c0, n = unit(i)
                dve.wait_ge(l2_up, i + 1)
                for b in range(b0, b0 + nb):
                    c = slice(b % 2 * S, (b % 2 + 1) * S)
                    last = V.tensor_scalar(ru[:, c], unit_ps[i][0:A2, 0, c], b1[:, b:b + 1], 0.0, ALU.add, ALU.max)
                linked(last)
                c = slice(c0, c0 + n)
                linked(V.tensor_copy(u[:, 0, c], ru[:, c]))
                V.tensor_tensor(u[:, 1, c], ru[:, c], u[:, 0, c].bitcast(f32), ALU.subtract).then_inc(l2_hid, 1)

            def res_stage(i):
                b0, nb, t0, c0, n = unit(i)
                dve.wait_ge(l2_down, i + 1)
                if i:
                    dve.wait_ge(x3_done, DT * min(i, 3))
                for dt in range(DT):
                    for b in range(b0, b0 + nb):
                        c = slice(b % 2 * S, (b % 2 + 1) * S)
                        last = V.scalar_tensor_tensor(y[:, dt, c], unit_ps[i][:, dt, c], b2c[:, b, dt:dt + 1],
                                                      x[:, dt, b * S:(b + 1) * S], ALU.add, ALU.add)
                    last.then_inc(centered, 1)

            def square_stage(i):
                b0, nb, t0, c0, n = unit(i)
                c = slice(c0, c0 + n)
                dve.wait_ge(centered, DT * (i + 1))
                V.tensor_tensor(sq[:, 1, c], y[:, 1, c], y[:, 1, c], ALU.mult).then_inc(sq_high, 1)

            def eps_stage(i):
                b0, nb, t0, c0, n = unit(i)
                dve.wait_ge(var_done, i + 1)
                qs = slice(c0 // P, (c0 + n) // P)
                V.tensor_scalar(var[:, qs], unit_ps[i][:, 1, qs], 1.0 / D, 1e-5, ALU.mult, ALU.add).then_inc(var_eps, 1)

            def diag_stage(i):
                b0, nb, t0, c0, n = unit(i)
                dve.wait_ge(rstd_done, i + 1)
                for q in range(c0 // P, (c0 + n) // P):
                    last = V.tensor_scalar(diag[:, q], ident[:], rstd[:, q:q + 1], None, ALU.mult)
                last.then_inc(diag_done, 1)

            def norm_stage(i):
                b0, nb, t0, c0, n = unit(i)
                c = slice(c0, c0 + n)
                dve.wait_ge(y_scaled, i + 1)
                dve.wait_ge(rstd_bc, i + 1)
                for dt in range(DT):
                    V.tensor_tensor(y[:, dt, c], unit_ps[i][:, 1, c], y[:, dt, c], ALU.mult).then_inc(normed, 1)

            def add_stage(i):
                b0, nb, t0, c0, n = unit(i)
                for dt in range(DT):
                    dve.wait_ge(normed, DT * i + dt + 1)
                    for b in range(b0, b0 + nb):
                        c = slice(b % 2 * S, (b % 2 + 1) * S)
                        xb = x[:, dt, b * S:(b + 1) * S]
                        last = V.scalar_tensor_tensor(xb, xb, cols[:, b, 4 + dt:5 + dt], y[:, dt, c], ALU.add, ALU.add)
                    last.then_inc(x3_done, 1)

            def out_stage(i, part):
                b0, nb, t0, c0, n = unit(i)
                half = n // P // 2
                q = c0 // P + part * half
                b = b0 + (q - c0 // P) // 2
                dve.wait_ge(l3_done, 2 * i + part + 1)
                if i >= 2 and not part:
                    dve.wait_ge(stored[i % 2], 32 * (i // 2))
                V.tensor_tensor(ostage[:, i % 2, q:q + half],
                                unit_ps[i][:, part, 0:half * D].rearrange("p (q n) -> p q n", q=half),
                                biasb[:, b:b + 1].to_broadcast([P, half, D]), ALU.add).then_inc(out_ready, 1)

            hooks = placed({"x2a": lambda i: unit_lo(x2_hi, x2_lo, i, 0), "x2b": lambda i: unit_lo(x2_hi, x2_lo, i, 1),
                            "hid": hid_stage, "res": res_stage, "square": square_stage, "eps": eps_stage,
                            "diag": diag_stage, "norm": norm_stage, "add": add_stage,
                            "x3a": lambda i: unit_lo(x3_hi, x3_lo, i, 0), "x3b": lambda i: unit_lo(x3_hi, x3_lo, i, 1),
                            "outa": lambda i: out_stage(i, 0), "outb": lambda i: out_stage(i, 1)})
            for b in range(B):
                hooks.setdefault(late_step(b), []).insert(0, lambda b=b: late_lo(b))
                hooks.setdefault(b, []).append(lambda b=b: center_w2(b))
            hooks.setdefault(10, []).insert(0, center_b2)

            def last_step(T, tok, N):
                sum_before = T % FT == 1 and T > 1
                l1_step(NE1 - 1, T, N, (NE1 - 1, T // FT - 1, *LAST_JOBS[T // FT - 1]) if sum_before else None)
                if T == 1:
                    l1_take(NE1 - 2, 3, 3 * BLK, BLK)

            last_steps(last_step, hooks)
            for T in range(40, 60):
                if T == 42:
                    l1_take(NE1 - 1, 4, *LAST_JOBS[4])
                for h in hooks.get(T, []):
                    h()


def kernel(**inputs):
    import numpy as np
    import concourse.bacc as bacc
    from concourse import mybir
    from concourse.bass_utils import run_bass_kernel_spmd

    v = {k: np.asarray(a) for k, a in inputs.items()}

    def by_rows(w):
        n = w.shape[0]
        return w.reshape(n, DT, P, FT, P).transpose(0, 2, 3, 1, 4).reshape(n, P, FT * D)

    def by_hidden(w):
        n = w.shape[0]
        return w.reshape(n, FT, P, D).transpose(0, 2, 1, 3).reshape(n, P, FT * D)

    def chunks(mats):
        s = np.stack([m.reshape(m.shape[0], P, 2, CH) for m in mats], axis=1)
        return s.transpose(0, 3, 1, 2, 4).reshape(-1, P, CH)

    shared = chunks([by_rows(v["L0_cond_share_wi"]), by_hidden(v["L0_cond_share_wo"])])
    ei = by_rows(v["L0_cond_expert_wi"]).reshape(4, P, 4, 512)
    eo = by_hidden(v["L0_cond_expert_wo"]).reshape(4, P, 4, 512)
    experts = np.concatenate([ei, eo], axis=3).transpose(0, 2, 1, 3).reshape(16, P, CH)
    cat = lambda a, b: np.concatenate([v[a], v[b][None]], axis=0)
    l1 = chunks([by_rows(cat("L1_cond_Wg", "L1_cond_Sg")), by_rows(cat("L1_cond_Wu", "L1_cond_Su")),
                 by_hidden(cat("L1_cond_Wd", "L1_cond_Sd"))])
    col = lambda a: a.reshape(-1, DT, P).transpose(0, 2, 1)
    arrays = {
        "xT": v["x"].reshape(B * S, DT, P).transpose(2, 1, 0),
        "shared": shared, "experts": experts, "l1": l1,
        "types": np.broadcast_to(v["itok_B_0_2"], (P, B)),
        "types_row": np.stack([v["itok_B_0_2"], v["itok_B_0_8"], v["itok_B_0_7"]]),
        "gvec": np.broadcast_to(v["L0_cond_gate_vecs"], (P, 3, 4)),
        "gw1": v["L0_cond_gate_w1"].reshape(8, P, D).transpose(1, 0, 2),
        "gw2": v["L0_cond_gate_w2"].reshape(2, P, 4).transpose(1, 0, 2),
        "prob": np.broadcast_to(v["fside_Bx8_0"], (P, B, 8)),
        "sgate": np.broadcast_to(v["condB_sharedgateprob"], (P, B)),
        "w1": v["L2_cond_W1"].reshape(-1, DT, P, A2).transpose(0, 2, 1, 3).reshape(-1, P, DT * A2),
        "w2": v["L2_cond_W2"],
        "b1": v["L2_cond_b1"][:, :, None],
        "cols": np.concatenate([col(v["L2_cond_b2"]), col(v["L2_cond_gamma"]), col(v["L2_cond_beta"])], axis=2),
        "w3": v["L3_cond_weight"].transpose(0, 2, 1).reshape(-1, DT, P, D).transpose(0, 2, 1, 3).reshape(-1, P, DT * D),
        "bias": v["L3_cond_bias"][:, None, :],
        "ident": np.eye(P, dtype=np.float32),
    }
    arrays = {f"in_{k}": np.ascontiguousarray(a) for k, a in arrays.items()}
    nc = bacc.Bacc("TRN2", target_bir_lowering=False, num_devices=1)
    ap = {k[3:]: nc.dram_tensor(k, a.shape, mybir.dt.from_np(a.dtype), kind="ExternalInput").ap()
          for k, a in arrays.items()}
    out = nc.dram_tensor("out", (B * S, D), mybir.dt.float32, kind="ExternalOutput").ap()
    build(nc, ap["xT"], ap["shared"], ap["experts"], ap["l1"], ap["types"], ap["types_row"], ap["gvec"], ap["gw1"],
          ap["gw2"], ap["prob"], ap["sgate"], ap["w1"], ap["w2"], ap["b1"], ap["cols"], ap["w3"],
          ap["bias"], ap["ident"], out)
    r = run_bass_kernel_spmd(nc, [arrays], core_ids=[0])
    return r.results[0]["out"].reshape(B, S, D)
```
